# Optimizing a Trainium2 kernel written in Bass

```python
import numpy as np
import jax
import jax.numpy as jnp

def _softmax(x, axis=-1):
    return jax.nn.softmax(x, axis=axis)

def _gelu(x):
    return jax.nn.gelu(x, approximate=True)

def _silu(x):
    return jax.nn.silu(x)

def _sigmoid(x):
    return jax.nn.sigmoid(x)

def _layernorm(x, axis=-1, eps=1e-05):
    m = jnp.mean(x, axis=axis, keepdims=True)
    v = jnp.var(x, axis=axis, keepdims=True)
    return (x - m) / jnp.sqrt(v + eps)

def _scatter_add(tgt, idx, src, axis=0):
    return tgt.at[idx].add(src)

def _segment_sum(src, seg, n):
    return jax.ops.segment_sum(src, seg, n)
kernel_name = 'mk_gnn_resnorm_d2_gnn_r8_fe4812'

def setup_inputs(seed: int=0):
    np.random.seed(seed)
    _w = jnp.asarray

    def _rec_inputs():
        import jax
        import jax.numpy as jnp
        _gk = jax.random.key(seed)
        x = -0.0002117 + 1 * jax.random.normal(jax.random.fold_in(_gk, 1), (12500, 256), jnp.float32)
        src = jax.random.randint(jax.random.fold_in(_gk, 2), (200000,), 0, 12500, jnp.int32)
        dst = jax.random.randint(jax.random.fold_in(_gk, 3), (200000,), 0, 12500, jnp.int32)
        _o = jnp.argsort(dst, stable=True)
        src = src[_o]
        dst = dst[_o]
        edge_weight = jax.random.uniform(jax.random.fold_in(_gk, 13), (200000,), jnp.float32, 0.0, 1)
        return (x, src, dst, edge_weight)
    x, src, dst, edge_weight = _rec_inputs()

    def _L0_gnn_setup():
        import jax, jax.numpy as jnp
        import numpy as np
        N = 12500
        E = 200000
        DIN = 256
        DOUT = 128
        H = 4
        DH = DOUT // H
        ORDER = 1
        EPS = 1e-09
        NEG_SLOPE = 0.2

        def _leaky(x):
            return jnp.where(x >= 0, x, NEG_SLOPE * x)
        key = jax.random.key(seed)
        ks = jax.random.split(key, 8)
        feat_in = jax.random.normal(ks[0], (N, DIN), jnp.float32)
        row = jax.random.randint(ks[1], (E,), 0, N)
        col = jax.random.randint(ks[2], (E,), 0, N)
        adj_vals = jax.random.uniform(ks[3], (E,), jnp.float32)
        W = jax.random.normal(ks[4], (ORDER + 1, H, DIN, DH), jnp.float32) * 0.05
        b = jnp.zeros((ORDER + 1, H, DH), jnp.float32)
        att = jax.random.normal(ks[5], (ORDER, H, 2 * DH), jnp.float32) * 0.05
        scale = jnp.ones((ORDER + 1, H, DH), jnp.float32)
        offset = jnp.zeros((ORDER + 1, H, DH), jnp.float32)
        return {'feat_in': feat_in, 'row': row, 'col': col, 'adj_vals': adj_vals, 'W': W, 'b': b, 'att': att, 'scale': scale, 'offset': offset}
    _L0_gnn_all = _L0_gnn_setup()
    _L0_gnn_in = {k: v for k, v in _L0_gnn_all.items() if k in ('W', 'b', 'att', 'scale', 'offset')}
    del _L0_gnn_all

    def _L1_gnn_setup():
        import jax, jax.numpy as jnp
        import numpy as np
        N_NODES = 1250
        N_EDGES = 40000
        IN_DIM = 256
        OUT_DIM = 256
        LN_EPS = 1e-05
        key = jax.random.key(seed)
        ks = jax.random.split(key, 4)
        x = jax.random.normal(ks[0], (N_NODES, IN_DIM), dtype=jnp.float32)
        edge_index = jax.random.randint(ks[1], (2, N_EDGES), 0, N_NODES, dtype=jnp.int64)
        W_msg = jax.random.normal(ks[2], (2 * IN_DIM, OUT_DIM), dtype=jnp.float32) / np.sqrt(2 * IN_DIM)
        b_msg = jnp.zeros((OUT_DIM,), dtype=jnp.float32)
        W_upd = jax.random.normal(ks[3], (IN_DIM + OUT_DIM, OUT_DIM), dtype=jnp.float32) / np.sqrt(IN_DIM + OUT_DIM)
        b_upd = jnp.zeros((OUT_DIM,), dtype=jnp.float32)
        gamma = jnp.ones((OUT_DIM,), dtype=jnp.float32)
        beta = jnp.zeros((OUT_DIM,), dtype=jnp.float32)
        return {'x': x, 'edge_index': edge_index, 'W_msg': W_msg, 'b_msg': b_msg, 'W_upd': W_upd, 'b_upd': b_upd, 'gamma': gamma, 'beta': beta}
    _L1_gnn_all = _L1_gnn_setup()
    _L1_gnn_in = {k: v for k, v in _L1_gnn_all.items() if k in ('W_msg', 'b_msg', 'W_upd', 'b_upd', 'gamma', 'beta')}
    del _L1_gnn_all
    return {'x': x, 'src': src, 'dst': dst, 'edge_weight': edge_weight, 'L0_gnn_W': _L0_gnn_in['W'], 'L0_gnn_b': _L0_gnn_in['b'], 'L0_gnn_att': _L0_gnn_in['att'], 'L0_gnn_scale': _L0_gnn_in['scale'], 'L0_gnn_offset': _L0_gnn_in['offset'], 'L1_gnn_W_msg': _L1_gnn_in['W_msg'], 'L1_gnn_b_msg': _L1_gnn_in['b_msg'], 'L1_gnn_W_upd': _L1_gnn_in['W_upd'], 'L1_gnn_b_upd': _L1_gnn_in['b_upd'], 'L1_gnn_gamma': _L1_gnn_in['gamma'], 'L1_gnn_beta': _L1_gnn_in['beta']}

def reference(x, src, dst, edge_weight, L0_gnn_W, L0_gnn_b, L0_gnn_att, L0_gnn_scale, L0_gnn_offset, L1_gnn_W_msg, L1_gnn_b_msg, L1_gnn_W_upd, L1_gnn_b_upd, L1_gnn_gamma, L1_gnn_beta):
    import jax
    import jax.numpy as jnp

    def _L0_gnn_ref(feat_in, row, col, adj_vals, W, b, att, scale, offset):
        import jax, jax.numpy as jnp
        import numpy as np
        N = 12500
        E = 200000
        DIN = 256
        DOUT = 128
        H = 4
        DH = DOUT // H
        ORDER = 1
        EPS = 1e-09
        NEG_SLOPE = 0.2

        def _leaky(x):
            return jnp.where(x >= 0, x, NEG_SLOPE * x)
        feat = jax.nn.relu(jnp.einsum('nd,ohdk->ohnk', feat_in, W) + b[:, :, None, :])
        feat_self = feat[0]
        feat_nei = feat[1]
        a_self, a_neigh = (att[0, :, :DH], att[0, :, DH:])
        att_s = _leaky(jnp.einsum('hnk,hk->hn', feat_self, a_self))
        att_n = _leaky(jnp.einsum('hnk,hk->hn', feat_nei, a_neigh))
        edge_w = (att_s[:, row] + att_n[:, col]) * adj_vals
        msgs = edge_w[..., None] * feat_nei[:, col, :]
        agg = jax.vmap(lambda m: jax.ops.segment_sum(m, row, num_segments=N))(msgs)
        feat = jnp.stack([feat_self, agg], axis=0)
        mean = feat.mean(axis=-1, keepdims=True)
        var = feat.var(axis=-1, keepdims=True) + EPS
        feat = (feat - mean) * scale[:, :, None, :] * jax.lax.rsqrt(var) + offset[:, :, None, :]
        per_order = feat.transpose(0, 2, 1, 3).reshape(ORDER + 1, N, H * DH)
        feat_out = jnp.concatenate([per_order[o] for o in range(ORDER + 1)], axis=1)
        return feat_out

    def _L1_gnn_ref(x, edge_index, W_msg, b_msg, W_upd, b_upd, gamma, beta):
        import jax, jax.numpy as jnp
        import numpy as np
        N_NODES = 1250
        N_EDGES = 40000
        IN_DIM = 256
        OUT_DIM = 256
        LN_EPS = 1e-05
        row, col = (edge_index[0], edge_index[1])
        msg_in = jnp.concatenate([x[row], x[col]], axis=-1)
        messages = jax.nn.relu(msg_in @ W_msg + b_msg)
        aggregated = jax.ops.segment_sum(messages, col, num_segments=x.shape[0])
        h = jax.nn.relu(jnp.concatenate([x, aggregated], axis=-1) @ W_upd + b_upd)
        mu = jnp.mean(h, axis=-1, keepdims=True)
        var = jnp.mean(jnp.square(h - mu), axis=-1, keepdims=True)
        return (h - mu) * jax.lax.rsqrt(var + LN_EPS) * gamma + beta
    edge_index = jnp.stack([src, dst])
    x = _layernorm(x + _L0_gnn_ref(x, src, dst, edge_weight, L0_gnn_W, L0_gnn_b, L0_gnn_att, L0_gnn_scale, L0_gnn_offset), axis=-1)
    x = _layernorm(x + _L1_gnn_ref(x, edge_index, L1_gnn_W_msg, L1_gnn_b_msg, L1_gnn_W_upd, L1_gnn_b_upd, L1_gnn_gamma, L1_gnn_beta), axis=-1)
    return x

_drawn_inputs = setup_inputs


def setup_inputs(seed=0):
    import zlib

    import numpy as np

    out = dict(_drawn_inputs(seed))
    spreads = {'L0_gnn_b': (0.0, 0.1),
     'L0_gnn_scale': (1.0, 0.2),
     'L0_gnn_offset': (0.0, 0.1),
     'L1_gnn_b_msg': (0.0, 0.1),
     'L1_gnn_b_upd': (0.0, 0.511),
     'L1_gnn_gamma': (1.0, 0.2),
     'L1_gnn_beta': (0.0, 0.1)}
    factors = {}
    for name, (base, spread) in spreads.items():
        noise = np.random.default_rng([zlib.crc32(name.encode()), seed]).standard_normal(out[name].shape)
        drawn = base * np.exp(spread * noise) if base else spread * noise
        out[name] = jnp.asarray(drawn.astype(out[name].dtype))
    for name, factor in factors.items():
        out[name] = (out[name] * factor).astype(out[name].dtype)
    return out
```

```python
import concourse.bass as bass
from concourse import mybir
from contextlib import ExitStack

f32 = mybir.dt.float32
i32 = mybir.dt.int32
ALU = mybir.AluOpType
ACT = mybir.ActivationFunctionType
AX = mybir.AxisListType

N = 12500
E = 200000
NT = 98
NP = 49
LASTR = N - 97 * 128
NROW = NT * 128
CH = 1563
CROWS = 1664
NS = 1664
NG = NS // 4
NC = 13
NACC = 4
C_ID, C_IO, C_LT, C_PID, C_STEP, C_DUMP = 0, 128, 256, 384, 385, 398
CW = 399


def wait(e, sem, v):
    if isinstance(v, int):
        if v > 0:
            e.wait_ge(sem, v)
    else:
        e.wait_ge(sem, v)


def drive(e, total, u, body, head=1, tail=0):
    mid = (total - tail) // u
    for j in range(head * u):
        body(j, j % u, j // u)
    with e.Fori(head, mid) as i:
        for g in range(u):
            body(i * u + g, g, i)
    for j in range(mid * u, total):
        body(j, j % u, j // u)


def uses(i, g, d, u):
    return i + ((g - d) // u + 1)


def gate(e, s):
    e.sem_inc(s, 1)


def known(j, *conditions):
    return isinstance(j, int) and any(f(j) for f in conditions)


def gnn(nc, x, src, dst, ew, W0, b0, att, scale, offset, Wm, bm, Wu, bu, gam, bet, cst, out):
    ctx = ExitStack()
    with ctx:
        def sb(name, shape, dt=f32):
            return ctx.enter_context(nc.sbuf_tensor(name, shape, dt))

        def sem(name):
            return ctx.enter_context(nc.semaphore(name))

        def dram(name, shape, dt=f32):
            return nc.dram_tensor(name, shape, dt).ap()

        srcT = dram("d_src", (CROWS, 128), i32)
        dstT = dram("d_dst", (CROWS, 128), i32)
        ewT = dram("d_ew", (CROWS, 128))
        d_tile = dram("d_tile", (NC, 128), i32)
        acc = [dram(f"d_acc{k}", (NROW + 128, 256)) for k in range(NACC)]
        d_xp = dram("d_xp", (NROW, 256))
        d_x1 = dram("d_x1", (NROW, 256))
        d_p = dram("d_p", (NROW, 256))
        d_q = dram("d_q", (NROW, 256))

        big = sb("big", [128, NT, 256])
        tab = sb("tab", [128, NG, 4, 4])
        c = sb("cstb", [128, CW])
        ats = sb("ats", [128, NT, 4])
        trow = sb("trow", [1, NS], i32)
        ident = c[:, C_ID:C_ID + 128]
        iota = c[:, C_IO:C_IO + 128]
        ltri = c[:, C_LT:C_LT + 128]
        ones = sb("ones", [128, 128])
        w0 = sb("w0", [128, 2, 256])
        brow = sb("brow", [1, 4, 256])
        attb = sb("attb", [128, 256])
        scb = sb("scb", [128, 256])
        ofb = sb("ofb", [128, 256])
        A = sb("arena", [128, 14336])
        win = sb("win", [128, 2, 4, 4])
        idx = sb("idx", [128, 4, 4], i32)
        small = sb("small", [128, 128])

        def carve():
            at = [0]

            def take(*shape):
                n = 1
                for s in shape:
                    n *= s
                v = A[:, at[0]:at[0] + n]
                at[0] += n
                assert at[0] <= 14336, at[0]
                names = "abcd"[:len(shape)]
                if len(shape) == 1:
                    return v
                return v.rearrange(f"p ({' '.join(names)}) -> p {' '.join(names)}",
                                   **{k: s for k, s in zip(names, shape)})
            return take

        PS = [ctx.enter_context(nc.psum_tensor(f"ps{i}", [128, 512], f32)) for i in range(8)]

        s_const = sem("s_const")
        s_gate = {q.engine: sem(f"s_gate{n}") for n, q in enumerate((nc.gpsimd, nc.vector))}
        s_w = sem("s_w")
        s_pad = sem("s_pad")
        s_tab = sem("s_tab")
        s_dl = sem("s_dl")
        s_zero = sem("s_zero")
        s_zm = sem("s_zm")
        s_A = sem("s_A")
        s_Ap = sem("s_Ap")
        s_Ag = sem("s_Ag")
        s_At = sem("s_At")
        s_tl = sem("s_tl")

        take = carve()
        dst_i = take(1600).bitcast(i32)
        dst_f = take(1600)
        junk = take(1600)
        cnt = take(100)
        gS = take(NC, 128)
        gD = take(NC, 128)
        gW = take(NC, 128)
        st = take(100)
        st_i = take(100).bitcast(i32)
        fi_i = take(100).bitcast(i32)
        la_i = take(100).bitcast(i32)
        fi = take(100)
        la = take(100)
        ne = take(100)
        bA = take(100)
        bB = take(100)
        dC = take(100)
        tS = take(NC)
        cS = take(NC)
        cI = take(NC).bitcast(i32)
        tI = take(NC).bitcast(i32)
        gj = take(100)
        gj2 = take(100)
        tfl = take(NC)
        zer = take(256)
        padi = take(128).bitcast(i32)
        padf = take(128)

        D = [sem(f"d_in{g}") for g in range(2)]
        d_tr = sem("d_tr")
        d_ac = sem("d_ac")
        d_mm = sem("d_mm")
        d_re = sem("d_re")
        d_fc = sem("d_fc")
        d_v = sem("d_v")
        d_lk = sem("d_lk")
        d_var = sem("d_var")
        d_sq = sem("d_sq")
        d_st = [sem(f"d_st{g}") for g in range(2)]
        s_end0 = sem("s_end0")

        e_win = sem("e_win")
        e_r = sem("e_r")
        e_oh = sem("e_oh")
        e_s = sem("e_s")
        e_sw = sem("e_sw")
        e_tt = sem("e_tt")
        e_ct = sem("e_ct")
        e_fl = sem("e_fl")
        e_ix = sem("e_ix")
        e_c = sem("e_c")
        e_cc = sem("e_cc")
        e_d = sem("e_d")
        e_dc = sem("e_dc")
        e_sc = [sem(f"e_sc{k}") for k in range(4)]

        B = [sem(f"b_in{g}") for g in range(2)]
        b_v = sem("b_v")
        b_var = sem("b_var")
        b_sq = sem("b_sq")
        b_x1 = sem("b_x1")
        b_tr = sem("b_tr")
        b_ac = sem("b_ac")
        b_mm = sem("b_mm")
        b_cp = sem("b_cp")
        b_st = [sem(f"b_st{g}") for g in range(2)]

        f_win = sem("f_win")
        f_ix = sem("f_ix")
        f_g = [sem(f"f_g{g}") for g in range(4)]
        f_q = [sem(f"f_q{g}") for g in range(4)]
        f_lb = sem("f_lb")
        f_oh = sem("f_oh")
        f_ot = sem("f_ot")
        f_qe = sem("f_qe")
        f_m = sem("f_m")
        f_re = sem("f_re")
        f_ag = sem("f_ag")
        f_acc = sem("f_acc")
        f_z = sem("f_z")

        G = [sem(f"g_in{g}") for g in range(2)]
        g_tr = sem("g_tr")
        g_ag = sem("g_ag")
        g_ac = sem("g_ac")
        g_mm = sem("g_mm")
        g_re = sem("g_re")
        g_v = sem("g_v")
        g_var = sem("g_var")
        g_sq = sem("g_sq")
        g_fin = sem("g_fin")
        g_st = [sem(f"g_st{g}") for g in range(2)]
        wm = sb("wm", [128, 2, 512])

        block = ctx.enter_context(nc.Block())

        def pair(t, j):
            return t[bass.ds(j * 256, 256), :].rearrange("(b p) c -> p b c", p=128)

        take = carve()
        X0 = [take(2, 256) for _ in range(2)]
        XT0 = [take(4, 128) for _ in range(2)]
        F0 = [take(2, 256) for _ in range(2)]
        U0 = take(2, 256)
        Z0 = take(2, 128)
        Y0 = take(2, 128)
        take = carve()
        OH = [take(4, 128) for _ in range(2)]
        SS = take(4, 128)
        SW = [take(4, 128) for _ in range(2)]
        TT = take(4, 128)
        CS = [take(4, 128) for _ in range(2)]
        DS = [take(4, 256) for _ in range(2)]
        take = carve()
        AC = [[take(2, 256) for _ in range(4)] for _ in range(2)]
        X1 = [take(2, 256) for _ in range(2)]
        U1 = take(2, 256)
        V1 = take(2, 256)
        Z1 = take(2, 128)
        Y1 = take(2, 128)
        XT1 = [take(4, 128) for _ in range(2)]
        PQ = [take(2, 512) for _ in range(2)]
        take = carve()
        OH1 = [take(4, 128) for _ in range(4)]
        OT1 = [take(4, 128) for _ in range(2)]
        G1 = [take(4, 256) for _ in range(4)]
        Q1 = [take(4, 256) for _ in range(2)]
        M1 = [take(4, 256) for _ in range(2)]
        take = carve()
        X2 = [take(2, 256) for _ in range(2)]
        XT2 = [take(8, 128) for _ in range(2)]
        H2 = [take(2, 256) for _ in range(2)]
        WU = take(4, 256)
        AG = [take(2, 256) for _ in range(2)]
        GB = take(256)
        BB = take(256)

        smp = small[:, :]

        @block.sync
        def _(e):
            e.dma_start(dst_i[0:125, :], dst.rearrange("(p c) -> p c", p=125)).then_inc(s_dl, 16)
            e.dma_start(c[:, :], cst).then_inc(s_const, 16)
            for t, s, q in ((srcT, src, padi), (dstT, dst, padi), (ewT, ew, padf)):
                e.dma_start(t[0:1562, :], s[0:1562 * 128].rearrange("(a b) -> a b", b=128)).then_inc(s_tab, 16)
                e.dma_start(t[1562:1563, 0:64], s[1562 * 128:E].rearrange("(a b) -> a b", a=1)).then_inc(s_tab, 16)
            e.wait_ge(s_pad, 4)
            for t, q in ((srcT, gS[:, 0, :].bitcast(i32)), (dstT, padi), (ewT, zer[:, 0:128])):
                e.dma_start(t[1562:1563, 64:128], q[0:1, 0:64]).then_inc(s_tab, 16)
                e.dma_start(t[1563:1664, :], q[0:101, :]).then_inc(s_tab, 16)
            for k in range(2):
                for o in range(2):
                    e.dma_start(w0[:, k, o * 128:(o + 1) * 128].rearrange("p (h d) -> p h d", h=4),
                                W0[o, :, k * 128:(k + 1) * 128, :].rearrange("h p d -> p h d")).then_inc(s_w, 16)
            e.dma_start(brow[:, 0, :], b0.rearrange("(a o) h d -> a (o h d)", a=1)).then_inc(s_w, 16)
            e.dma_start(brow[:, 1, :], bm.rearrange("(a n) -> a n", a=1)).then_inc(s_w, 16)
            e.dma_start(brow[:, 2, :], bu.rearrange("(a n) -> a n", a=1)).then_inc(s_w, 16)
            e.dma_start(wm[:, :, 0:256], Wm[0:256, :].rearrange("(k p) n -> p k n", p=128)).then_inc(s_w, 16)
            e.dma_start(wm[:, :, 256:512], Wm[256:512, :].rearrange("(k p) n -> p k n", p=128)).then_inc(s_w, 16)
            for o in range(2):
                e.dma_start(attb[:, o * 128:(o + 1) * 128].rearrange("p (h d) -> p h d", h=4),
                            att[0:1, :, o * 32:(o + 1) * 32].to_broadcast([128, 4, 32])).then_inc(s_w, 16)
            e.dma_start(scb[:, :], scale.rearrange("(a o) h d -> a (o h d)", a=1).to_broadcast([128, 256])).then_inc(s_w, 16)
            e.dma_start(ofb[:, :], offset.rearrange("(a o) h d -> a (o h d)", a=1).to_broadcast([128, 256])).then_inc(s_w, 16)
            e.wait_ge(s_A, A_TILE)
            e.dma_start(d_tile.rearrange("c p -> p c"), tI, allow_slow_non_contiguous=True).then_inc(s_tl, 16)
            e.wait_ge(s_tl, 16)
            e.dma_start(trow[:, :].rearrange("a (c p) -> a c p", c=NC), d_tile.rearrange("(a c) p -> a c p", a=1)).then_inc(s_tl, 16)

            e.wait_ge(s_At, A_END)

            def load(j, g, i):
                wait(e, d_st[g], 16 * uses(i, g, 2, 2))
                last = isinstance(j, int) and j == NP - 1
                if last:
                    e.dma_start(X0[g][:, 0, :], x[j * 256:j * 256 + 128, :]).then_inc(D[g], 16)
                    e.dma_start(X0[g][0:LASTR, 1, :], x[j * 256 + 128:N, :]).then_inc(D[g], 16)
                else:
                    e.dma_start(X0[g][:, 0, :], x[bass.ds(j * 256, 128), :]).then_inc(D[g], 16)
                    e.dma_start(X0[g][:, 1, :], x[bass.ds(j * 256 + 128, 128), :]).then_inc(D[g], 16)
            drive(e, NP, 2, load, tail=1)

            e.wait_ge(s_end0, 1)
            for k in range(4):
                e.wait_ge(e_sc[k], 16 * NG)

            def loadb(j, g, i):
                wait(e, b_st[g], 48 * uses(i, g, 2, 2))
                for k in range(4):
                    e.dma_start(AC[g][k], pair(acc[k], j)).then_inc(B[g], 16)
                e.dma_start(X1[g], pair(d_xp, j)).then_inc(B[g], 16)
            drive(e, NP, 2, loadb, tail=1)

            e.wait_ge(b_st[0], 48 * 25)
            e.wait_ge(b_st[1], 48 * 24)
            regs = [e.alloc_register(f"spt{k}") for k in range(4)]

            def loadq(j, g, i):
                wait(e, f_qe, j - 1)
                e.load(regs, trow[0:1, bass.ds(j * 4, 4)])
                for k in range(4):
                    t = e.snap(regs[k], min_val=0, max_val=NT - 1)
                    e.dma_start(Q1[g % 2][:, k, :], d_q[bass.ds(t * 128, 128), :]).then_inc(f_q[g], 16)
            drive(e, NG, 4, loadq)

            e.wait_ge(f_acc, 4 * NG)
            e.dma_start(WU, Wu.rearrange("(k p) n -> p k n", p=128)).then_inc(s_w, 16)
            e.dma_start(GB, gam.rearrange("(a n) -> a n", a=1).to_broadcast([128, 256])).then_inc(s_w, 16)
            e.dma_start(BB, bet.rearrange("(a n) -> a n", a=1).to_broadcast([128, 256])).then_inc(s_w, 16)

            def loadg(j, g, i):
                wait(e, g_st[g], 16 * uses(i, g, 2, 2))
                e.dma_start(X2[g], pair(d_x1, j)).then_inc(G[g], 16)
            drive(e, NP, 2, loadg, tail=1)

        @block.gpsimd
        def _(e):
            e.memset(zer, 0.0).then_inc(s_pad, 1)
            e.memset(padi, -1).then_inc(s_pad, 1)
            e.memset(gS[:, 0, :].bitcast(i32), 0).then_inc(s_pad, 1)
            e.memset(ones[:, :], 1.0).then_inc(s_pad, 1)
            e.wait_ge(s_A, A_CHUNK)
            e.wait_ge(s_tab, 16 * 12)
            for cc in range(NC):
                for t, d in ((srcT, gS.bitcast(i32)), (dstT, gD.bitcast(i32)), (ewT, gW)):
                    e.indirect_dma_start(out=d[:, cc, :], out_offset=None, in_=t,
                                         in_offset=bass.IndirectOffsetOnAxis(ap=cI[:, cc:cc + 1], axis=0)).then_inc(s_Ag, 16)

            for k in range(NACC):
                e.wait_ge(s_zero, 16 * NACC)

            def scat(j, g, i):
                wait(e, e_dc, 2 * (j + 1))
                wait(e, e_ix, j + 1)
                for k in range(4):
                    wait(e, e_sc[k], j * 16)
                    gate(e, s_gate[e.engine])
                    e.indirect_dma_start(out=acc[k], out_offset=bass.IndirectOffsetOnAxis(ap=idx[:, g, k:k + 1], axis=0),
                                         in_=DS[g % 2][:, k, :], in_offset=None, compute_op=ALU.add).then_inc(e_sc[k], 16)
            drive(e, NG, 4, scat)
            for k in range(4):
                e.wait_ge(e_sc[k], 16 * NG)

            def gath(j, g, i):
                wait(e, f_ix, j + 1)
                wait(e, f_m, 2 * (j - 3))
                for k in range(4):
                    gate(e, s_gate[e.engine])
                    e.indirect_dma_start(out=G1[g][:, k, :], out_offset=None, in_=d_p,
                                         in_offset=bass.IndirectOffsetOnAxis(ap=idx[:, g, k:k + 1], axis=0)).then_inc(f_g[g], 16)
            drive(e, NG, 4, gath)

            def sums(j, g, i):
                if known(j, lambda j: j == 0):
                    e.wait_ge(f_acc, 4 * NG)
                wait(e, g_tr, j - 1)
                e.wait_ge(f_acc, 4 * NG)
                e.tensor_copy(AG[g], big[:, bass.ds(2 * j, 2), :]).then_inc(g_ag, 1)
            drive(e, NP, 2, sums, tail=1)

        @block.scalar
        def _(e):
            e.wait_ge(s_pad, 4)
            for k in range(NACC):
                e.dma_start(acc[k][0:NROW, :].rearrange("(b p) c -> p b c", p=128),
                            zer.unsqueeze(1).to_broadcast([128, NT, 256])).then_inc(s_zero, 16)
            for n in range(3 * NC):
                e.wait_ge(s_Ap, n + 2)
                kind, cc = n // NC, n % NC
                e.activation(tab[:, cc * 32:(cc + 1) * 32, kind, :],
                             PS[n % 2][:, 0:128].rearrange("p (a b) -> p a b", b=4), ACT.Copy).then_inc(s_At, 1)

            def dense(j, g, i):
                if not known(j, lambda j: j >= NP):
                    wait(e, d_mm, j - 1)
                    wait(e, d_tr, j + 1)
                    e.activation(XT0[g], PS[g][:, :].rearrange("p (a b) -> p a b", a=4), ACT.Copy).then_inc(d_ac, 1)
                    wait(e, d_v, 12 * (j - 1))
                    wait(e, d_fc, j - 1)
                    wait(e, d_mm, j + 1)
                    e.activation(F0[g], PS[2 + g][:, :].rearrange("p (a b) -> p a b", a=2), ACT.Relu).then_inc(d_re, 1)
                    wait(e, d_re, j + 1)
                    e.wait_ge(s_pad, 4)
                    e.activation(big[:, bass.ds(2 * j, 2), 0:128], F0[g][:, :, 128:256], ACT.Copy).then_inc(d_fc, 1)
                if not known(j, lambda j: j < 1):
                    wait(e, d_var, j)
                    e.activation(smp[:, 40:48], smp[:, 32:40], ACT.Sqrt).then_inc(d_sq, 1)
                    wait(e, d_v, 12 * j)
                    e.dma_start(pair(d_xp, j - 1), X0[1 - g]).then_inc(d_st[1 - g], 16)
            drive(e, NP + 1, 2, dense, tail=2)
            e.wait_ge(d_st[0], 16 * 25)
            e.wait_ge(d_st[1], 16 * 24)
            e.wait_ge(d_fc, NP)
            e.sem_inc(s_end0, 1)

            def edge0(j, g, i):
                if not (known(j, lambda j: j < 1, lambda j: j > NG)):
                    wait(e, e_c, j)
                    wait(e, e_d, j - 2)
                    e.activation(CS[(g - 1) % 2], PS[2 + (g - 1) % 2][:, :].rearrange("p (a b) -> p a b", a=4),
                                 ACT.Copy).then_inc(e_cc, 1)
                if not (isinstance(j, int) and j < 2):
                    for k in range(4):
                        wait(e, e_sc[k], (j - 3) * 16)
                    for h in range(2):
                        wait(e, e_d, j - 1)
                        e.activation(DS[g % 2][:, 2 * h:2 * h + 2, :],
                                     PS[4 + 2 * (g % 2) + h][:, :].rearrange("p (a b) -> p a b", a=2),
                                     ACT.Copy).then_inc(e_dc, 1)
            drive(e, NG + 2, 4, edge0, tail=2)

            def densb(j, g, i):
                o = 1 - g
                if not known(j, lambda j: j >= NP):
                    wait(e, b_var, 2 * j + 1)
                    e.activation(smp[:, 40:48], smp[:, 32:40], ACT.Sqrt).then_inc(b_sq, 1)
                if not known(j, lambda j: j < 1):
                    wait(e, b_mm, j - 2)
                    wait(e, b_tr, j)
                    e.activation(XT1[o], PS[o][:, :].rearrange("p (a b) -> p a b", a=4), ACT.Copy).then_inc(b_ac, 1)
                if not known(j, lambda j: j >= NP):
                    wait(e, b_var, 2 * j + 2)
                    e.activation(smp[:, 60:62], smp[:, 56:58], ACT.Sqrt).then_inc(b_sq, 1)
                if not known(j, lambda j: j < 1):
                    wait(e, b_st[o], 48 * uses(i, g, 3, 2))
                    wait(e, b_mm, j)
                    for b in range(2):
                        e.activation(PQ[o][:, b, :], PS[2 + 2 * o + b][:, :], ACT.Copy).then_inc(b_cp, 1)
                    wait(e, b_cp, 2 * j)
                    wait(e, b_x1, j)
                    e.dma_start(pair(d_p, j - 1), PQ[o][:, :, 0:256]).then_inc(b_st[o], 16)
                    e.dma_start(pair(d_q, j - 1), PQ[o][:, :, 256:512]).then_inc(b_st[o], 16)
                    e.dma_start(pair(d_x1, j - 1), X1[o]).then_inc(b_st[o], 16)
            drive(e, NP + 1, 2, densb, tail=2)
            e.wait_ge(b_st[0], 48 * 25)
            e.wait_ge(b_st[1], 48 * 24)

            def edge1(j, g, i):
                if not (isinstance(j, int) and j < 1):
                    wait(e, f_m, 2 * j)
                    e.activation(M1[(g - 1) % 2], M1[(g - 1) % 2], ACT.Relu).then_inc(f_re, 1)
            drive(e, NG + 1, 4, edge1, tail=1)

            def densg(j, g, i):
                o = 1 - g
                if not known(j, lambda j: j >= NP):
                    wait(e, g_mm, j - 1)
                    wait(e, g_tr, j + 1)
                    for b in range(2):
                        e.activation(XT2[g][:, 4 * b:4 * b + 4, :], PS[2 * g + b][:, :].rearrange("p (a b) -> p a b", a=4),
                                     ACT.Copy).then_inc(g_ac, 1)
                    wait(e, g_st[g], 16 * uses(i, g, 2, 2))
                    wait(e, g_mm, j + 1)
                    e.activation(H2[g], PS[4 + g][:, :].rearrange("p (a b) -> p a b", a=2), ACT.Relu).then_inc(g_re, 1)
                if not known(j, lambda j: j < 1):
                    for s in range(2):
                        wait(e, g_var, 2 * j + s - 1)
                        e.activation(smp[:, 60:62], smp[:, 56:58], ACT.Sqrt).then_inc(g_sq, 1)
                    wait(e, g_fin, j)
                    if known(j, lambda j: j == NP):
                        e.dma_start(out[(j - 1) * 256:j * 256 - 128, :], H2[o][:, 0, :]).then_inc(g_st[o], 16)
                        e.dma_start(out[j * 256 - 128:N, :], H2[o][0:LASTR, 1, :]).then_inc(g_st[o], 16)
                    else:
                        e.dma_start(out[bass.ds((j - 1) * 256, 256), :].rearrange("(b p) c -> p b c", p=128), H2[o]).then_inc(g_st[o], 16)
            drive(e, NP + 1, 2, densg, tail=2)
            e.wait_ge(g_st[0], 16 * 26)
            e.wait_ge(g_st[1], 16 * 24)

        @block.tensor
        def _(e):
            e.wait_ge(s_pad, 4)
            e.wait_ge(s_A, A_CNT)
            e.matmul(PS[7][:, 0:100], ones[0:125, :], cnt[0:125, :], start=True, stop=True).then_inc(s_Ap, 1)
            e.wait_ge(s_const, 16)
            for n in range(3 * NC):
                kind, cc = n // NC, n % NC
                e.wait_ge(s_A, A_LOC)
                if n >= 2:
                    e.wait_ge(s_At, n - 1)
                e.transpose(PS[n % 2][:, 0:128], (gD, gS, gW)[kind][:, cc, :], ident).then_inc(s_Ap, 1)

            e.wait_ge(s_w, 16 * 13)

            def dense(j, g, i):
                wait(e, D[g], 32 * uses(i, g, 0, 2))
                wait(e, d_ac, j - 1)
                for b in range(2):
                    for k in range(2):
                        m = e.transpose(PS[g][:, (2 * b + k) * 128:(2 * b + k + 1) * 128],
                                        X0[g][:, b, k * 128:(k + 1) * 128], ident)
                m.then_inc(d_tr, 1)
                wait(e, d_ac, j + 1)
                wait(e, d_re, j - 1)
                for b in range(2):
                    o = PS[2 + g][:, b * 256:(b + 1) * 256]
                    for k in range(2):
                        e.matmul(o, XT0[g][:, 2 * b + k, :], w0[:, k, :], start=(k == 0), stop=False)
                    m = e.matmul(o, ones[0:1, :], brow[0:1, 0, :], start=False, stop=True)
                m.then_inc(d_mm, 1)
            drive(e, NP, 2, dense, tail=1)
            e.wait_ge(s_end0, 1)
            e.wait_ge(s_tl, 32)
            regs = [e.alloc_register(f"pet{k}") for k in range(4)]

            def edge0(j, g, i):
                if not (isinstance(j, int) and j >= NG):
                    wait(e, e_win, j + 1)
                    wait(e, e_s, j - 1)
                    for k in range(4):
                        m = e.transpose(PS[g % 2][:, k * 128:(k + 1) * 128],
                                        win[:, g % 2, 1, k:k + 1].to_broadcast([128, 128]), ident)
                    m.then_inc(e_r, 1)
                if not (known(j, lambda j: j < 1, lambda j: j > NG)):
                    wait(e, e_sw, j)
                    wait(e, e_oh, j)
                    wait(e, e_cc, j - 2)
                    q = (g - 1) % 2
                    for k in range(4):
                        m = e.matmul(PS[2 + q][:, k * 128:(k + 1) * 128], OH[q][:, k, :], SW[q][:, k, :], start=True, stop=True)
                    m.then_inc(e_c, 1)
                if not (isinstance(j, int) and j < 2):
                    q = g % 2
                    e.load(regs, trow[0:1, bass.ds(j * 4 - 8, 4)])
                    wait(e, e_cc, j - 1)
                    wait(e, e_dc, 2 * (j - 3))
                    for k in range(4):
                        t = e.snap(regs[k], min_val=0, max_val=NT - 1)
                        m = e.matmul(PS[4 + 2 * q + k // 2][:, (k % 2) * 256:(k % 2) * 256 + 256],
                                     CS[q][:, k, :], big[:, t, :], start=True, stop=True)
                    m.then_inc(e_d, 1)
            drive(e, NG + 2, 4, edge0, tail=2)

            def densb(j, g, i):
                wait(e, b_x1, j + 1)
                wait(e, b_ac, j - 1)
                for b in range(2):
                    for k in range(2):
                        m = e.transpose(PS[g][:, (2 * b + k) * 128:(2 * b + k + 1) * 128],
                                        X1[g][:, b, k * 128:(k + 1) * 128], ident)
                m.then_inc(b_tr, 1)
                wait(e, b_ac, j + 1)
                wait(e, b_cp, 2 * (j - 1))
                for b in range(2):
                    o = PS[2 + 2 * g + b]
                    for k in range(2):
                        e.matmul(o[:, :], XT1[g][:, 2 * b + k, :], wm[:, k, :], start=(k == 0), stop=False)
                    m = e.matmul(o[:, 0:256], ones[0:1, :], brow[0:1, 1, :], start=False, stop=True)
                m.then_inc(b_mm, 1)
            drive(e, NP, 2, densb, tail=1)
            e.wait_ge(b_cp, 2 * NP)

            def edge1(j, g, i):
                if not (isinstance(j, int) and j >= NG):
                    wait(e, f_win, j + 1)
                    wait(e, f_ot, j - 1)
                    for k in range(4):
                        m = e.transpose(PS[g % 2][:, k * 128:(k + 1) * 128],
                                        win[:, g % 2, 0, k:k + 1].to_broadcast([128, 128]), ident)
                    m.then_inc(f_lb, 1)
                if not (known(j, lambda j: j < 1, lambda j: j > NG)):
                    q = (g - 1) % 2
                    wait(e, f_ot, j)
                    g1 = (g - 1) % 4
                    wait(e, f_q[g1], 64 * uses(i, g, 1, 4))
                    wait(e, f_m, 2 * (j - 2))
                    for k in range(4):
                        m = e.matmul(PS[2 + 2 * q + k // 2][:, (k % 2) * 256:(k % 2) * 256 + 256],
                                     OT1[q][:, k, :], Q1[q][:, k, :], start=True, stop=True)
                    m.then_inc(f_qe, 1)
                if not (isinstance(j, int) and j < 2):
                    q = g % 2
                    wait(e, f_re, j - 1)
                    wait(e, f_oh, j - 1)
                    wait(e, f_acc, 4 * (j - 2))
                    for k in range(4):
                        m = e.matmul(PS[6 + k // 2][:, (k % 2) * 256:(k % 2) * 256 + 256],
                                     OH1[(g - 2) % 4][:, k, :], M1[q][:, k, :], start=True, stop=True)
                    m.then_inc(f_ag, 1)
            drive(e, NG + 2, 4, edge1, tail=2)
            e.wait_ge(s_w, 16 * 16)

            def densg(j, g, i):
                wait(e, G[g], 16 * uses(i, g, 0, 2))
                wait(e, g_ag, j + 1)
                wait(e, g_ac, 2 * (j - 1))
                for b in range(2):
                    for k in range(4):
                        s = X2[g][:, b, k * 128:(k + 1) * 128] if k < 2 else AG[g][:, b, (k - 2) * 128:(k - 1) * 128]
                        m = e.transpose(PS[2 * g + b][:, k * 128:(k + 1) * 128], s, ident)
                m.then_inc(g_tr, 1)
                wait(e, g_ac, 2 * j + 2)
                wait(e, g_re, j - 1)
                for b in range(2):
                    o = PS[4 + g][:, b * 256:(b + 1) * 256]
                    for k in range(4):
                        e.matmul(o, XT2[g][:, 4 * b + k, :], WU[:, k, :], start=(k == 0), stop=False)
                    m = e.matmul(o, ones[0:1, :], brow[0:1, 2, :], start=False, stop=True)
                m.then_inc(g_mm, 1)
            drive(e, NP, 2, densg, tail=1)

        @block.vector
        def _(e):
            n = [0]

            def A1(ins):
                n[0] += 1
                ins.then_inc(s_A, 1)
                e.wait_ge(s_A, n[0])

            e.wait_ge(s_dl, 16)
            A1(e.tensor_copy(dst_f[0:125, :], dst_i[0:125, :]))
            A1(e.memset(cnt[:, :], 0.0))
            for t in range(1, NT):
                A1(e.tensor_scalar(junk[0:125, :], dst_f[0:125, :], float(128 * t), 0.0, ALU.is_lt, ALU.add,
                                   accum_out=cnt[0:125, t:t + 1]))
            A1(e.memset(cnt[0:125, NT:NT + 1], float(E // 125)))
            assert n[0] == A_CNT
            e.wait_ge(s_Ap, 1)
            A1(e.tensor_copy(st, PS[7][:, 0:100]))
            A1(e.tensor_copy(st_i, st))
            A1(e.tensor_scalar(fi_i, st_i, 7, None, ALU.arith_shift_right))
            A1(e.tensor_scalar(bA, st, 127.0, None, ALU.add))
            A1(e.tensor_copy(la_i, bA))
            A1(e.tensor_scalar(st_i, la_i, 7, None, ALU.arith_shift_right))
            A1(e.tensor_copy(fi, fi_i))
            A1(e.tensor_copy(la, st_i))
            A1(e.tensor_tensor(ne[:, 0:NT], st[:, 1:NT + 1], st[:, 0:NT], ALU.is_gt))
            A1(e.tensor_tensor(dC[:, 0:NT], la[:, 1:NT + 1], fi[:, 0:NT], ALU.subtract))
            A1(e.memset(bA, 0.0))
            A1(e.tensor_tensor(bA[:, 1:NT], dC[:, 0:NT - 1], ne[:, 0:NT - 1], ALU.mult))
            a, b = bA, bB
            for k in range(7):
                d = 1 << k
                A1(e.tensor_copy(b[:, 0:d], a[:, 0:d]))
                A1(e.tensor_tensor(b[:, d:NT], a[:, d:NT], a[:, 0:NT - d], ALU.add))
                a, b = b, a
            A1(e.tensor_tensor(la[:, 0:NT], fi[:, 0:NT], a[:, 0:NT], ALU.subtract))
            A1(e.tensor_tensor(dC[:, 1:NT], la[:, 1:NT], la[:, 0:NT - 1], ALU.subtract))
            e.wait_ge(s_const, 16)
            for cc in range(NC):
                s = c[:, C_STEP + cc:C_STEP + cc + 1]
                A1(e.tensor_scalar(gj[:, 1:NT], a[:, 1:NT], s, 0.0, ALU.is_le, ALU.add, accum_out=tS[:, cc:cc + 1]))
                A1(e.tensor_tensor(gj2[:, 1:NT], gj[:, 1:NT], dC[:, 1:NT], ALU.mult))
                A1(e.tensor_reduce(cS[:, cc:cc + 1], gj2[:, 1:NT], AX.X, ALU.add))
            A1(e.tensor_copy(tI, tS))
            assert n[0] == A_TILE
            A1(e.tensor_tensor(tfl, cS, c[:, C_STEP:C_STEP + NC], ALU.add))
            A1(e.tensor_scalar(cS, tfl, float(CH), None, ALU.min))
            A1(e.tensor_copy(cI, cS))
            assert n[0] == A_CHUNK
            A1(e.tensor_scalar(tfl, tS, 128.0, None, ALU.mult))
            e.wait_ge(s_Ag, 16 * 3 * NC)
            A1(e.tensor_copy(gS, gS.bitcast(i32)))
            A1(e.tensor_tensor(gD, gD.bitcast(i32), tfl.unsqueeze(2).to_broadcast([128, NC, 128]), ALU.subtract))
            assert n[0] == A_LOC
            e.wait_ge(s_At, 3 * NC)
            e.tensor_scalar(tab[:, :, 3, :], tab[:, :, 1, :], c[:, C_DUMP:C_DUMP + 1], -1.0, ALU.subtract, ALU.mult).then_inc(s_At, 1)

            e.wait_ge(s_w, 16 * 13)
            hb = [128, 2, 4, 32]

            def h4(ap):
                return ap.rearrange("p b (h d) -> p b h d", h=4)

            def bc2(ap):
                return ap.unsqueeze(1).to_broadcast([128, 2, ap.shape[1]])

            def norm_heads(e, V, src4, out4, xc, sq, half, var, sq_sem, j, nth):
                V(e.tensor_reduce(smp[:, 0:8].rearrange("p (b h) -> p b h", b=2), src4, AX.X, ALU.add))
                V(e.tensor_scalar(smp[:, 8:16], smp[:, 0:8], 1.0 / 32, None, ALU.mult))
                V(e.tensor_tensor(h4(xc), src4, smp[:, 8:16].rearrange("p (b h) -> p b h", b=2).unsqueeze(3).to_broadcast(hb), ALU.subtract))
                V(e.tensor_tensor(sq, xc, xc, ALU.mult))
                V(e.tensor_reduce(smp[:, 16:24].rearrange("p (b h) -> p b h", b=2), h4(sq), AX.X, ALU.add))
                e.tensor_scalar(smp[:, 32:40], smp[:, 16:24], 1.0 / 32, 1e-9, ALU.mult, ALU.add).then_inc(var, 1)
                sq_sem()
                V(e.reciprocal(smp[:, 48:56], smp[:, 40:48]))
                V(e.tensor_tensor(h4(sq), h4(xc), smp[:, 48:56].rearrange("p (b h) -> p b h", b=2).unsqueeze(3).to_broadcast(hb), ALU.mult))
                V(e.tensor_tensor(xc, sq, bc2(scb[:, half * 128:half * 128 + 128]), ALU.mult))
                V(e.tensor_tensor(sq, xc, bc2(ofb[:, half * 128:half * 128 + 128]), ALU.add))

            def dense(j, g, i):
                k = [0]

                def V(ins):
                    k[0] += 1
                    ins.then_inc(d_v, 1)
                    wait(e, d_v, 12 * j + k[0])

                wait(e, d_re, j + 1)
                V(e.tensor_tensor(U0, F0[g], bc2(attb[:, :]), ALU.mult))
                V(e.tensor_reduce(smp[:, 64:80].rearrange("p (b h) -> p b h", b=2),
                                  U0.rearrange("p b (h d) -> p b h d", h=8), AX.X, ALU.add))
                e.scalar_tensor_tensor(smp[:, 80:96], smp[:, 64:80], 0.2, smp[:, 64:80], ALU.mult, ALU.max).then_inc(d_lk, 1)
                wait(e, d_lk, j + 1)
                e.tensor_copy(ats[:, bass.ds(2 * j, 2), :], smp[:, 80:96].rearrange("p (b o h) -> p b o h", b=2, o=2)[:, :, 0, :])
                e.tensor_tensor(big[:, bass.ds(2 * j, 2), 128:256].rearrange("p b (h d) -> p b h d", h=4),
                                F0[g][:, :, 128:256].rearrange("p b (h d) -> p b h d", h=4),
                                smp[:, 80:96].rearrange("p (b o h) -> p b o h", b=2, o=2)[:, :, 1, :].unsqueeze(3).to_broadcast(hb), ALU.mult)

                def rs():
                    wait(e, d_sq, j + 1)
                norm_heads(e, V, h4(F0[g][:, :, 0:128]), None, Y0, Z0, 0, d_var, rs, j, 0)
                wait(e, D[g], 32 * uses(i, g, 0, 2))
                wait(e, d_tr, j + 1)
                k[0] += 1
                e.tensor_tensor(X0[g][:, :, 0:128], X0[g][:, :, 0:128], Z0, ALU.add).then_inc(d_v, 1)
                assert k[0] == 12, k[0]
                wait(e, d_v, 12 * j + 12)
            drive(e, NP, 2, dense, tail=1)
            e.wait_ge(s_end0, 1)
            e.wait_ge(s_At, 3 * NC + 1)

            def window(j, g, s, after):
                e.tensor_copy(win[:, g % 2, :, :], tab[:, j, :, :]).then_inc(s, 1)

            window(0, 0, e_win, None)
            b4 = [128, 4, 128]

            def edge0(j, g, i):
                q = g % 2
                if not (isinstance(j, int) and j >= NG - 1):
                    wait(e, e_ix, j)
                    wait(e, e_r, j)
                    window(j + 1, g + 1, e_win, None)
                wait(e, e_win, j + 1)
                wait(e, e_c, j - 1)
                e.tensor_tensor(OH[q], iota.unsqueeze(1).to_broadcast(b4),
                                win[:, q, 0, :].unsqueeze(2).to_broadcast(b4), ALU.is_equal).then_inc(e_oh, 1)
                wait(e, e_r, j + 1)
                e.tensor_tensor(SS, PS[q][:, :].rearrange("p (a b) -> p a b", a=4),
                                win[:, q, 1, :].unsqueeze(2).to_broadcast(b4), ALU.is_equal).then_inc(e_s, 1)
                wait(e, e_s, j + 1)
                e.tensor_tensor(SW[q], SS, win[:, q, 2, :].unsqueeze(2).to_broadcast(b4), ALU.mult).then_inc(e_sw, 1)
                e.tensor_tensor(TT, SS, ltri.unsqueeze(1).to_broadcast(b4), ALU.mult).then_inc(e_tt, 1)
                wait(e, e_tt, j + 1)
                e.tensor_reduce(smp[:, 96:100], TT, AX.X, ALU.add).then_inc(e_ct, 1)
                wait(e, e_ct, j + 1)
                e.scalar_tensor_tensor(smp[:, 100:104], smp[:, 96:100], 0.5, win[:, q, 3, :], ALU.is_gt, ALU.mult).then_inc(e_fl, 1)
                wait(e, e_fl, j + 1)
                for k in range(4):
                    wait(e, e_sc[k], (j - 3) * 16)
                e.tensor_tensor(idx[:, g, :], smp[:, 100:104], win[:, q, 1, :], ALU.add).then_inc(e_ix, 1)
            drive(e, NG, 4, edge0, tail=1)
            for k in range(4):
                e.wait_ge(e_sc[k], 16 * NG)

            def densb(j, g, i):
                k = [0]
                NV = 21

                def V(ins):
                    k[0] += 1
                    ins.then_inc(b_v, 1)
                    wait(e, b_v, NV * j + k[0])

                wait(e, B[g], 80 * uses(i, g, 0, 2))
                V(e.tensor_tensor(U1, AC[g][0], AC[g][1], ALU.add))
                V(e.tensor_tensor(V1, AC[g][2], AC[g][3], ALU.add))
                V(e.tensor_tensor(AC[g][0], U1, V1, ALU.add))
                V(e.tensor_tensor(h4(Y1), h4(AC[g][0][:, :, 0:128]),
                                  ats[:, bass.ds(2 * j, 2), :].unsqueeze(3).to_broadcast(hb), ALU.mult))
                V(e.tensor_tensor(U1[:, :, 0:128], Y1, AC[g][0][:, :, 128:256], ALU.add))

                def rs():
                    wait(e, b_sq, 2 * j + 1)
                norm_heads(e, V, h4(U1[:, :, 0:128]), None, Y1, Z1, 1, b_var, rs, j, 0)
                V(e.tensor_tensor(X1[g][:, :, 128:256], X1[g][:, :, 128:256], Z1, ALU.add))
                for b in range(2):
                    V(e.bn_stats(smp[:, 104 + 6 * b:110 + 6 * b], X1[g][:, b, :]))
                for b in range(2):
                    gate(e, s_gate[e.engine])
                    V(e.bn_aggr(smp[:, 116 + 2 * b:118 + 2 * b], smp[:, 104 + 6 * b:110 + 6 * b]))
                e.tensor_scalar(smp[:, 56:58], smp[:, 116:120].rearrange("p (b t) -> p b t", t=2)[:, :, 1], 1e-5, None, ALU.add).then_inc(b_var, 1)
                wait(e, b_sq, 2 * j + 2)
                V(e.reciprocal(smp[:, 62:64], smp[:, 60:62]))
                V(e.tensor_scalar(X1[g][:, 0, :], X1[g][:, 0, :], smp[:, 116:117], smp[:, 62:63], ALU.subtract, ALU.mult))
                assert k[0] == NV, k[0]
                e.tensor_scalar(X1[g][:, 1, :], X1[g][:, 1, :], smp[:, 118:119], smp[:, 63:64],
                                ALU.subtract, ALU.mult).then_inc(b_x1, 1)
                wait(e, b_x1, j + 1)
            drive(e, NP, 2, densb, tail=1)

            e.wait_ge(b_st[0], 48 * 25)
            e.wait_ge(b_st[1], 48 * 24)
            e.memset(big[:, :, :], 0.0).then_inc(f_z, 1)
            e.wait_ge(f_z, 1)

            def window1(j, g):
                e.tensor_copy(win[:, g % 2, :, :], tab[:, j, :, :]).then_inc(f_win, 1)
                e.tensor_copy(idx[:, g % 4, :], tab[:, j, 1, :]).then_inc(f_ix, 1)
            window1(0, 0)
            window1(1, 1)

            def accs(j, g):
                e.load(regs, trow[0:1, bass.ds(j * 4 - 8, 4)])
                ts = [e.snap(r, min_val=0, max_val=NT - 1) for r in regs]
                wait(e, f_ag, j - 1)
                for k, t in enumerate(ts):
                    wait(e, f_acc, (j - 2) * 4 + k)
                    e.tensor_tensor(big[:, t, :], big[:, t, :],
                                    PS[6 + k // 2][:, (k % 2) * 256:(k % 2) * 256 + 256], ALU.add).then_inc(f_acc, 1)
            regs = [e.alloc_register(f"dvt{k}") for k in range(4)]

            def edge1(j, g, i):
                q = g % 2
                real = not (isinstance(j, int) and j >= NG)
                if real:
                    wait(e, f_lb, j + 1)
                    wait(e, f_win, j + 1)
                    wait(e, f_qe, j - 1)
                    e.tensor_scalar(OT1[q], PS[q][:, :].rearrange("p (a b) -> p a b", a=4), c[:, C_PID:C_PID + 1], None,
                                    ALU.is_equal).then_inc(f_ot, 1)
                    wait(e, f_ag, j - 3)
                    e.tensor_tensor(OH1[g], iota.unsqueeze(1).to_broadcast(b4),
                                    win[:, q, 0, :].unsqueeze(2).to_broadcast(b4), ALU.is_equal).then_inc(f_oh, 1)
                    if not (isinstance(j, int) and j >= NG - 2):
                        wait(e, f_oh, j + 1)
                        g2 = (g + 2) % 4
                        wait(e, f_g[g2], 64 * uses(i, g, 2, 4))
                        window1(j + 2, g + 2)
                if not (known(j, lambda j: j < 1, lambda j: j > NG)):
                    p = (g - 1) % 2
                    g1 = (g - 1) % 4
                    wait(e, f_qe, j)
                    wait(e, f_ag, j - 2)
                    wait(e, f_g[g1], 64 * uses(i, g, 1, 4))
                    for h in range(2):
                        e.tensor_tensor(M1[p][:, 2 * h:2 * h + 2, :], G1[g1][:, 2 * h:2 * h + 2, :],
                                              PS[2 + 2 * p + h][:, :].rearrange("p (a b) -> p a b", a=2), ALU.add).then_inc(f_m, 1)
                if not (isinstance(j, int) and j < 2):
                    accs(j, g)
            drive(e, NG + 2, 4, edge1, tail=6)
            e.wait_ge(f_acc, 4 * NG)

            e.wait_ge(s_w, 16 * 16)

            def ln(V, buf, var, sqs, j, s):
                for b in range(2):
                    V(e.bn_stats(smp[:, 104 + 6 * b:110 + 6 * b], buf[:, b, :]))
                for b in range(2):
                    gate(e, s_gate[e.engine])
                    V(e.bn_aggr(smp[:, 116 + 2 * b:118 + 2 * b], smp[:, 104 + 6 * b:110 + 6 * b]))
                e.tensor_scalar(smp[:, 56:58], smp[:, 116:120].rearrange("p (b t) -> p b t", t=2)[:, :, 1], 1e-5, None, ALU.add).then_inc(var, 1)
                wait(e, sqs, 2 * j + s + 1)
                V(e.reciprocal(smp[:, 62:64], smp[:, 60:62]))

            def densg(j, g, i):
                k = [0]
                NV = 16

                def V(ins):
                    k[0] += 1
                    ins.then_inc(g_v, 1)
                    wait(e, g_v, NV * j + k[0])
                wait(e, g_re, j + 1)
                ln(V, H2[g], g_var, g_sq, j, 0)
                for b in range(2):
                    V(e.tensor_scalar(H2[g][:, b, :], H2[g][:, b, :], smp[:, 116 + 2 * b:117 + 2 * b], smp[:, 62 + b:63 + b],
                                      ALU.subtract, ALU.mult))
                V(e.tensor_tensor(H2[g], H2[g], bc2(GB), ALU.mult))
                V(e.tensor_tensor(H2[g], H2[g], bc2(BB), ALU.add))
                wait(e, G[g], 16 * uses(i, g, 0, 2))
                V(e.tensor_tensor(H2[g], H2[g], X2[g], ALU.add))
                ln(V, H2[g], g_var, g_sq, j, 1)
                V(e.tensor_scalar(H2[g][:, 0, :], H2[g][:, 0, :], smp[:, 116:117], smp[:, 62:63], ALU.subtract, ALU.mult))
                e.tensor_scalar(H2[g][:, 1, :], H2[g][:, 1, :], smp[:, 118:119], smp[:, 63:64],
                                ALU.subtract, ALU.mult).then_inc(g_fin, 1)
                wait(e, g_fin, j + 1)
                assert k[0] == NV, k[0]
            drive(e, NP, 2, densg, tail=1)


A_CNT = 2 + (NT - 1) + 1
A_TILE = A_CNT + 12 + 14 + 2 + 3 * NC + 1
A_CHUNK = A_TILE + 3
A_LOC = A_CHUNK + 3
A_END = 3 * NC + 1

_INS = ['x', 'src', 'dst', 'edge_weight', 'L0_gnn_W', 'L0_gnn_b', 'L0_gnn_att', 'L0_gnn_scale', 'L0_gnn_offset',
        'L1_gnn_W_msg', 'L1_gnn_b_msg', 'L1_gnn_W_upd', 'L1_gnn_b_upd', 'L1_gnn_gamma', 'L1_gnn_beta']


def constants():
    import numpy as np
    c = np.zeros((128, CW), np.float32)
    p = np.arange(128, dtype=np.float32)
    c[:, C_ID:C_ID + 128] = np.eye(128)
    c[:, C_IO:C_IO + 128] = p[None, :]
    c[:, C_LT:C_LT + 128] = p[None, :] < p[:, None]
    c[:, C_PID] = p
    c[:, C_STEP:C_STEP + NC] = p[:, None] + 128 * np.arange(NC, dtype=np.float32)[None, :]
    c[:, C_DUMP] = NROW + p
    return c


def kernel(**inputs):
    import numpy as _np
    import concourse.bacc as _bacc
    from concourse import mybir as _mybir
    from concourse.bass_utils import run_bass_kernel_spmd as _run

    nc = _bacc.Bacc("TRN2", target_bir_lowering=False, num_devices=1)
    arrays, args = {}, []
    for name in _INS:
        a = _np.ascontiguousarray(inputs[name])
        arrays[f"in_{name}_dram"] = a
        args.append(nc.dram_tensor(f"in_{name}_dram", a.shape, _mybir.dt.from_np(a.dtype), kind="ExternalInput").ap())
    a = constants()
    arrays["in_cst_dram"] = a
    args.append(nc.dram_tensor("in_cst_dram", a.shape, _mybir.dt.from_np(a.dtype), kind="ExternalInput").ap())
    args.append(nc.dram_tensor("out_0_dram", (N, 256), f32, kind="ExternalOutput").ap())
    gnn(nc, *args)
    r = _run(nc, [arrays], core_ids=[0])
    return r.results[0]["out_0_dram"]
```

```python
import concourse.bass as bass
from concourse import mybir
from contextlib import ExitStack

f32 = mybir.dt.float32
i32 = mybir.dt.int32
bf16 = mybir.dt.bfloat16
ALU = mybir.AluOpType
ACT = mybir.ActivationFunctionType
AX = mybir.AxisListType

N = 12500
E = 200000
NT = 98
NP = 49
LASTR = N - 97 * 128
NROW = NT * 128
CH = 1563
CROWS = 1664
NS = 1664
NG = NS // 4
NC = 13
NACC = 4
C_ID, C_IO, C_LT, C_PID, C_STEP, C_DUMP = 0, 128, 256, 384, 385, 398
CW = 399


SHARED = {"b_" + n: ("d_" + n, NP) for n in ("hs", "me", "mm", "rc", "rv", "s2", "sc", "sq", "var", "x", "xc", "z")}
SHARED.update({"g_" + n: ("d_" + m, NP) for n, m in (("re", "re"), ("gm", "gm"), ("at", "fc"), ("ag", "xo"), ("xb", "lk"),
                                                     ("tr", "u"))})
SHARED.update({"g_" + n: ("d_" + m, 2 * NP) for n, m in (("mm", "mm"), ("sq", "sq"), ("add", "x"), ("r1", "rc"), ("v1", "var"))})
SHARED.update({"g_" + n: ("b_" + n, NP) for n in ("rn", "sr", "r2", "v2")})
SHARED.update({"g_" + n: ("b_" + m, 2 * NP) for n, m in (("n1", "nm"), ("b1", "bn"), ("a1", "ag"))})


def wait(e, sem, v):
    if isinstance(v, int):
        if v > 0:
            e.wait_ge(sem, v)
    else:
        e.wait_ge(sem, v)


def drive(e, total, u, body, head=1, tail=0):
    mid = (total - tail) // u
    for j in range(head * u):
        body(j, j % u, j // u)
    with e.Fori(head, mid) as i:
        for g in range(u):
            body(i * u + g, g, i)
    for j in range(mid * u, total):
        body(j, j % u, j // u)


def uses(i, g, d, u):
    return i + ((g - d) // u + 1)


def gate(e, s):
    e.sem_inc(s, 1)


def uses2(i, g, d):
    return i * 2 + ((g - d) // 2 + 1)


def known(j, *conditions):
    return isinstance(j, int) and any(f(j) for f in conditions)


def gnn(nc, x, xT, src, dst, ew, W0, b0, att, scale, offset, Wm, bm, Wu, bu, gam, bet, cst, out):
    ctx = ExitStack()
    with ctx:
        def sb(name, shape, dt=f32):
            return ctx.enter_context(nc.sbuf_tensor(name, shape, dt))

        sems = {}

        def S(name):
            name = SHARED[name][0] if name in SHARED else name
            if name not in sems:
                sems[name] = ctx.enter_context(nc.semaphore("q_" + name))
            return sems[name]

        def base(name):
            return SHARED[name][1] if name in SHARED else 0

        def waitn(e, name, v):
            if not isinstance(v, int) or v > 0:
                e.wait_ge(S(name), v + base(name))
                if e is nc.sync and not isinstance(v, int):
                    go(e)

        def dram(name, shape, dt=f32):
            return nc.dram_tensor(name, shape, dt).ap()

        srcT = dram("d_src", (CROWS, 128), i32)
        dstT = dram("d_dst", (CROWS, 128), i32)
        ewT = dram("d_ew", (CROWS, 128))
        d_tile = dram("d_tile", (NC, 128), i32)
        acc = [dram(f"d_acc{k}", (NROW + 128, 256)) for k in range(NACC)]
        d_xp = dram("d_xp", (NROW, 256))
        d_x1 = dram("d_x1", (NROW, 256))
        d_xt = dram("d_xt", (NP * 128, 512))
        d_p = dram("d_p", (NROW, 256))
        d_q = dram("d_q", (NROW, 256))

        big = sb("big", [128, NT, 256])
        tab = sb("tab", [128, NG, 4, 4])
        c = sb("cstb", [128, CW])
        ats = sb("ats", [128, NT, 4])
        trow = sb("trow", [1, NS], i32)
        ident = c[:, C_ID:C_ID + 128]
        iota = c[:, C_IO:C_IO + 128]
        ltri = c[:, C_LT:C_LT + 128]
        ones = sb("ones", [128, 128])
        onesb = sb("onesb", [3, 128], bf16)
        b3 = sb("b3", [3, 3, 256], bf16)
        w0 = sb("w0", [128, 2, 256])
        attb = sb("attb", [128, 256])
        scb = sb("scb", [128, 256])
        ofb = sb("ofb", [128, 256])
        A = sb("arena", [128, AW])
        win = sb("win", [128, 4, 4, 4])
        idx = sb("idx", [128, 4, 4], i32)
        small = sb("small", [128, 4, 112])
        wm = sb("wm", [128, 2, 512])

        def carve(buf, start=0):
            at = [start]

            def take(*shape):
                n = 1
                for s in shape:
                    n *= s
                v = buf[:, at[0]:at[0] + n]
                at[0] += n
                assert at[0] <= buf.shape[1], at[0]
                if len(shape) == 1:
                    return v
                names = "abcd"[:len(shape)]
                return v.rearrange(f"p ({' '.join(names)}) -> p {' '.join(names)}",
                                   **{k: s for k, s in zip(names, shape)})
            return take

        PS = [ctx.enter_context(nc.psum_tensor(f"ps{i}", [128, 512], f32)) for i in range(8)]

        s_const, s_w, s_pad, s_tab, s_dl, s_zero = (S(n) for n in ("const", "w", "pad", "tab", "dl", "zero"))
        s_A = S("A")
        s_Ap, s_Ag, s_At, s_Ac, s_tl = (S(n) for n in ("Ap", "Ag", "At", "Ac", "tl"))
        s_gate = {q.engine: S(f"gate{n}") for n, q in enumerate((nc.gpsimd, nc.vector, nc.scalar, nc.sync))}

        def go(e):
            gate(e, s_gate[e.engine])

        take = carve(big[:, :, :].rearrange("p a b -> p (a b)"))
        dst_i = take(1600).bitcast(i32)
        dst_f = take(1600)
        nxt_i = take(1600).bitcast(i32)
        nxt_f = take(1600)
        junk = take(1600)
        sid_i = take(1600).bitcast(i32)
        tid_f = take(1600)
        tid_b = take(800).bitcast(bf16)
        junkb = take(800).bitcast(bf16)
        junka = take(1600)
        fsrc = take(1600)
        few = take(1600)
        fO, fR, fM, fB = take(NT), take(NT), take(NT), take(NT)
        fcol, fpos = take(1), take(1)
        fpi = take(1).bitcast(i32)
        fval = take(3)
        brow = take(3, 256)
        bpart = take(3, 256)
        brem = take(3, 256)
        bsum = take(3, 256)
        bbf = take(3, 128).bitcast(bf16)
        take = carve(A)
        gS = take(NC, 128)
        gD = take(NC, 128)
        gW = take(NC, 128)
        zer = take(256)
        padi = take(128).bitcast(i32)
        cnt = take(100)
        sgn = take(100)
        thr = take(100)
        st, fi, la, ne, bA, bB, dC, gj, gj2 = (take(100) for _ in range(9))
        st_i, fi_i, la_i, le_i = (take(100).bitcast(i32) for _ in range(4))
        tS, cS, tfl = (take(NC) for _ in range(3))
        cI, tI = (take(NC).bitcast(i32) for _ in range(2))
        X0 = [take(2, 256) for _ in range(4)]
        F0 = [take(2, 256) for _ in range(2)]
        U0 = take(2, 256)
        XC0 = [take(2, 128) for _ in range(2)]
        SQ0 = [take(2, 128) for _ in range(2)]
        Z0 = [take(2, 128) for _ in range(2)]
        Y0 = [take(2, 128) for _ in range(2)]
        take = carve(tab[:, :, :, :].rearrange("p a b c -> p (a b c)"))
        XT0 = [take(2, 256) for _ in range(4)]
        take = carve(A)
        OH = [take(4, 128) for _ in range(2)]
        SS = take(4, 128)
        SW = [take(4, 128) for _ in range(2)]
        TT = take(4, 128)
        CS = [take(4, 128) for _ in range(2)]
        DS = [take(4, 256) for _ in range(2)]
        take = carve(A)
        AC = [[take(2, 256) for _ in range(4)] for _ in range(2)]
        X1 = [take(2, 256) for _ in range(4)]
        XN = [take(2, 256) for _ in range(2)]
        XT1 = [take(4, 128) for _ in range(2)]
        PQ = [take(2, 512) for _ in range(2)]
        SA = take(2, 256)
        YB = take(2, 128)
        VV = take(2, 128)
        XC1 = [take(2, 128) for _ in range(2)]
        SQ1 = [take(2, 128) for _ in range(2)]
        Z1 = take(2, 128)
        Z2 = take(2, 128)
        take = carve(A)
        OH1 = [take(4, 128) for _ in range(4)]
        OT1 = [take(4, 128) for _ in range(2)]
        G1 = [take(4, 256) for _ in range(4)]
        Q1 = [take(4, 256) for _ in range(2)]
        M1 = [take(4, 256) for _ in range(2)]
        take = carve(A)
        X2 = [take(2, 256) for _ in range(4)]
        XT2 = [take(4, 128) for _ in range(2)]
        AG = [take(2, 256) for _ in range(2)]
        AT = [take(4, 128) for _ in range(2)]
        H2 = [take(2, 256) for _ in range(2)]
        N2 = [take(2, 256) for _ in range(2)]
        O2 = [take(2, 256) for _ in range(2)]
        WU = take(4, 256)
        GB = take(256)
        BB = take(256)

        def pair(t, j):
            return t[bass.ds(j * 256, 256), :].rearrange("(b p) c -> p b c", p=128)

        def sm(g, a, n):
            return small[:, g % 4, a:a + n]

        def bc2(ap):
            return ap.unsqueeze(1).to_broadcast([128, 2, ap.shape[1]])

        hb = [128, 2, 4, 32]
        b4 = [128, 4, 128]

        def h4(ap):
            return ap.rearrange("p b (h d) -> p b h d", h=4)

        def bh(ap):
            return ap.rearrange("p (b h) -> p b h", b=2)

        def q4(ap):
            return ap.rearrange("p (a b) -> p a b", a=4)

        def q2(ap):
            return ap.rearrange("p (a b) -> p a b", a=2)

        def done(j, last, lag=0):
            return isinstance(j, int) and not 0 <= j - lag < last

        block = ctx.enter_context(nc.Block())

        def stored_b(e):
            for h, n in ((0, 25), (1, 24)):
                e.wait_ge(S(f"b_s1{h}"), 16 * n)
                e.wait_ge(S(f"b_s2{h}"), 16 * n)
                e.wait_ge(S(f"b_s3{h}"), 32 * n)

        def unsorted(e, name, body):
            r = e.alloc_register(name)
            e.load([r], st_i[0:1, 99:100])
            with e.If_ne(r, 0):
                body()

        @block.sync
        def _(e):
            e.dma_start(dst_i[0:125, :], dst.rearrange("(p c) -> p c", p=125)).then_inc(s_dl, 16)
            e.dma_start(nxt_i[0:124, :], dst[1:1 + 124 * 1600].rearrange("(p c) -> p c", p=124)).then_inc(s_dl, 16)
            e.dma_start(nxt_i[124:125, 0:1599], dst[1 + 124 * 1600:E].rearrange("(a c) -> a c", a=1)).then_inc(s_dl, 16)
            e.dma_start(nxt_i[124:125, 1599:1600], dst[E - 1:E].rearrange("(a c) -> a c", a=1)).then_inc(s_dl, 16)
            e.dma_start(c[:, :], cst).then_inc(s_const, 16)
            for t, s in ((srcT, src), (dstT, dst), (ewT, ew)):
                e.dma_start(t[0:1562, :], s[0:1562 * 128].rearrange("(a b) -> a b", b=128)).then_inc(s_tab, 16)
                e.dma_start(t[1562:1563, 0:64], s[1562 * 128:E].rearrange("(a b) -> a b", a=1)).then_inc(s_tab, 16)
            e.wait_ge(s_pad, 3)
            for t, q in ((srcT, zer[:, 0:128].bitcast(i32)), (dstT, padi), (ewT, zer[:, 0:128])):
                e.dma_start(t[1562:1563, 64:128], q[0:1, 0:64]).then_inc(s_tab, 16)
                e.dma_start(t[1563:1664, :], q[0:101, :]).then_inc(s_tab, 16)
            for n, b in enumerate((b0.rearrange("(a o) h d -> a (o h d)", a=1), bm.rearrange("(a n) -> a n", a=1),
                                   bu.rearrange("(a n) -> a n", a=1))):
                e.dma_start(brow[0:3, n, :], b.to_broadcast([3, 256])).then_inc(s_w, 16)
            for k in range(2):
                for o in range(2):
                    e.dma_start(w0[:, k, o * 128:(o + 1) * 128].rearrange("p (h d) -> p h d", h=4),
                                W0[o, :, k * 128:(k + 1) * 128, :].rearrange("h p d -> p h d")).then_inc(s_w, 16)
            e.dma_start(wm[:, :, 0:256], Wm[0:256, :].rearrange("(k p) n -> p k n", p=128)).then_inc(s_w, 16)
            e.dma_start(wm[:, :, 256:512], Wm[256:512, :].rearrange("(k p) n -> p k n", p=128)).then_inc(s_w, 16)
            for o in range(2):
                e.dma_start(attb[:, o * 128:(o + 1) * 128].rearrange("p (h d) -> p h d", h=4),
                            att[0:1, :, o * 32:(o + 1) * 32].to_broadcast([128, 4, 32])).then_inc(s_w, 16)
            e.dma_start(scb[:, :], scale.rearrange("(a o) h d -> a (o h d)", a=1).to_broadcast([128, 256])).then_inc(s_w, 16)
            e.dma_start(ofb[:, :], offset.rearrange("(a o) h d -> a (o h d)", a=1).to_broadcast([128, 256])).then_inc(s_w, 16)

            def load(j, g, i):
                if not done(j, NP):
                    waitn(e, "d_mm", j - 3)
                    waitn(e, f"d_st{g}", 16 * uses(i, g, 4, 4))
                    if known(j, lambda j: j == NP - 1):
                        e.dma_start(XT0[g][:, :, 0:128 + LASTR],
                                    xT.rearrange("(k p) n -> p k n", p=128)[:, :, j * 256:N]).then_inc(S(f"d_xt{g}"), 16)
                        e.dma_start(X0[g][:, 0, :], x[j * 256:j * 256 + 128, :]).then_inc(S(f"d_in{g}"), 16)
                        e.dma_start(X0[g][0:LASTR, 1, :], x[j * 256 + 128:N, :]).then_inc(S(f"d_in{g}"), 16)
                    else:
                        e.dma_start(XT0[g], xT.rearrange("(k p) n -> p k n", p=128)[:, :, bass.ds(j * 256, 256)])\
                         .then_inc(S(f"d_xt{g}"), 16)
                        e.dma_start(X0[g], pair(x, j)).then_inc(S(f"d_in{g}"), 16)
                if not done(j, NP, 3):
                    waitn(e, "d_x", j - 2)
                    e.dma_start(pair(d_xp, j - 3), X0[(g - 3) % 4]).then_inc(S(f"d_st{(g - 3) % 4}"), 16)
            drive(e, NP + 3, 4, load, tail=4)

            e.wait_ge(s_A, A_TILE)
            e.dma_start(d_tile.rearrange("c p -> p c"), tI, allow_slow_non_contiguous=True).then_inc(s_tl, 16)
            e.wait_ge(s_tl, 16)
            e.dma_start(trow[:, :].rearrange("a (c p) -> a c p", c=NC), d_tile.rearrange("(a c) p -> a c p", a=1)).then_inc(s_tl, 16)

            for g in range(4):
                e.wait_ge(S(f"d_st{g}"), 16 * (13 if g == 0 else 12))
            for k in range(4):
                e.wait_ge(S(f"e_sc{k}"), 16 * NG)

            def loadb(j, g, i):
                h = g % 2
                if not done(j, NP):
                    waitn(e, "b_v", j - 1)
                    for k in range(4):
                        e.dma_start(AC[h][k], pair(acc[k], j)).then_inc(S(f"b_ac{h}"), 16)
                    waitn(e, "b_nm", 2 * (j - 3))
                    e.dma_start(X1[g], pair(d_xp, j)).then_inc(S(f"b_in{g}"), 16)
                if not done(j, NP, 4):
                    waitn(e, "b_nm", 2 * (j - 3))
                    e.dma_start(pair(d_x1, j - 4), XN[h]).then_inc(S(f"b_s1{h}"), 16)
                if not done(j, NP, 5):
                    waitn(e, "b_xt", j - 4)
                    e.dma_start(d_xt[bass.ds((j - 5) * 128, 128), :], XT1[1 - h].rearrange("p a b -> p (a b)"))\
                     .then_inc(S(f"b_s2{1 - h}"), 16)
                if not done(j, NP, 6):
                    waitn(e, "b_pq", 2 * (j - 5))
                    e.dma_start(pair(d_p, j - 6), PQ[h][:, :, 0:256]).then_inc(S(f"b_s3{h}"), 16)
                    e.dma_start(pair(d_q, j - 6), PQ[h][:, :, 256:512]).then_inc(S(f"b_s3{h}"), 16)
            drive(e, NP + 6, 4, loadb, head=2, tail=7)
            stored_b(e)

            regs = [e.alloc_register(f"spt{k}") for k in range(4)]

            def loadq(j, g, i):
                e.load(regs, trow[0:1, bass.ds(j * 4, 4)])
                ts = [e.snap(r, min_val=0, max_val=NT - 1) for r in regs]
                waitn(e, "f_qe", j - 1)
                for k, t in enumerate(ts):
                    e.dma_start(Q1[g % 2][:, k, :], d_q[bass.ds(t * 128, 128), :]).then_inc(S(f"f_q{g}"), 16)
            drive(e, NG, 4, loadq)

            e.wait_ge(S("f_acc"), 4 * NG)
            e.dma_start(WU, Wu.rearrange("(k p) n -> p k n", p=128)).then_inc(s_w, 16)
            e.dma_start(GB, gam.rearrange("(a n) -> a n", a=1).to_broadcast([128, 256])).then_inc(s_w, 16)
            e.dma_start(BB, bet.rearrange("(a n) -> a n", a=1).to_broadcast([128, 256])).then_inc(s_w, 16)

            def loadg(j, g, i):
                h = g % 2
                if not done(j, NP):
                    waitn(e, "g_mm", j - 1)
                    e.dma_start(XT2[h].rearrange("p a b -> p (a b)"), d_xt[bass.ds(j * 128, 128), :]).then_inc(S(f"g_xt{h}"), 16)
                    waitn(e, "g_add", j - 3)
                    e.dma_start(X2[g], pair(d_x1, j)).then_inc(S(f"g_in{g}"), 16)
                if not done(j, NP, 5):
                    waitn(e, "g_n2", 2 * (j - 4))
                    o = O2[1 - h]
                    if known(j, lambda j: j - 5 == NP - 1):
                        e.dma_start(out[(j - 5) * 256:(j - 5) * 256 + 128, :], o[:, 0, :]).then_inc(S(f"g_st{1 - h}"), 16)
                        e.dma_start(out[(j - 5) * 256 + 128:N, :], o[0:LASTR, 1, :]).then_inc(S(f"g_st{1 - h}"), 16)
                    else:
                        e.dma_start(pair(out, j - 5), o).then_inc(S(f"g_st{1 - h}"), 16)
            drive(e, NP + 5, 4, loadg, head=2, tail=6)
            e.wait_ge(S("g_st0"), 16 * 26)
            e.wait_ge(S("g_st1"), 16 * 24)

        @block.gpsimd
        def _(e):
            e.memset(zer, 0.0).then_inc(s_pad, 1)
            e.memset(padi, -1).then_inc(s_pad, 1)
            e.memset(ones[:, :], 1.0).then_inc(s_pad, 1)
            e.wait_ge(s_tab, 16 * 12)
            e.wait_ge(s_A, A_FLAG)

            def place():
                e.dma_start(fsrc[0:125, :], src.rearrange("(p c) -> p c", p=125).bitcast(f32)).then_inc(S("u_l"), 16)
                e.dma_start(few[0:125, :], ew.rearrange("(p c) -> p c", p=125)).then_inc(S("u_l"), 16)

                def one(j, g, i):
                    waitn(e, "u_pi", j + 1)
                    waitn(e, "u_v", j + 1)
                    go(e)
                    for k, t in enumerate((dstT, srcT, ewT)):
                        v = fval[0:125, k:k + 1]
                        e.indirect_dma_start(out=t.rearrange("a (b o) -> (a b) o", o=1),
                                             out_offset=bass.IndirectOffsetOnAxis(ap=fpi[0:125, :], axis=0),
                                             in_=v if k == 2 else v.bitcast(i32), in_offset=None).then_inc(S(f"u_sc{k}"), 16)
                drive(e, 1600, 1, one)
                for k in range(3):
                    e.wait_ge(S(f"u_sc{k}"), 16 * 1600)
            unsorted(e, "pool_u", place)

            e.wait_ge(s_A, A_CHUNK)
            for cc in range(NC):
                for t, d in ((srcT, gS.bitcast(i32)), (dstT, gD.bitcast(i32)), (ewT, gW)):
                    e.indirect_dma_start(out=d[:, cc, :], out_offset=None, in_=t,
                                         in_offset=bass.IndirectOffsetOnAxis(ap=cI[:, cc:cc + 1], axis=0)).then_inc(s_Ag, 16)
            e.wait_ge(s_w, 16 * 13)

            def dense(j, g, i):
                h = g % 2
                if not done(j, NP):
                    waitn(e, f"d_in{g}", 16 * uses(i, g, 0, 4) + (16 if known(j, lambda j: j == NP - 1) else 0))
                    e.tensor_tensor(X0[g], X0[g], bc2(ofb[:, :]), ALU.add).then_inc(S("d_xo"), 1)
                    waitn(e, "d_re", j + 1)
                    waitn(e, "d_lk", j + 1)
                    go(e)
                    e.tensor_tensor(h4(big[:, bass.ds(2 * j, 2), 128:256]), h4(F0[h][:, :, 128:256]),
                                    sm(g, 16, 16).rearrange("p (b o h) -> p b o h", b=2, o=2)[:, :, 1, :].unsqueeze(3).to_broadcast(hb),
                                    ALU.mult).then_inc(S("d_gm"), 1)
                if not done(j, NP, 2):
                    waitn(e, "d_x", j - 3)
                    waitn(e, "d_z", j - 1)
                    e.tensor_tensor(Y0[h], Z0[h], bc2(scb[:, 0:128]), ALU.mult).then_inc(S("d_sc"), 1)
            drive(e, NP + 2, 4, dense, tail=3)

            e.wait_ge(s_zero, 16 * NACC)

            def scat(j, g, i):
                waitn(e, "e_dc", 2 * (j + 1))
                waitn(e, "e_ix", j + 1)
                for k in range(4):
                    waitn(e, f"e_sc{k}", j * 16)
                    go(e)
                    e.indirect_dma_start(out=acc[k], out_offset=bass.IndirectOffsetOnAxis(ap=idx[:, g, k:k + 1], axis=0),
                                         in_=DS[g % 2][:, k, :], in_offset=None, compute_op=ALU.add).then_inc(S(f"e_sc{k}"), 16)
            drive(e, NG, 4, scat)
            for k in range(4):
                e.wait_ge(S(f"e_sc{k}"), 16 * NG)

            def dense1(j, g, i):
                h = g % 2
                waitn(e, f"b_ac{h}", 64 * uses2(i, g, 0))
                e.tensor_tensor(AC[h][0], AC[h][0], AC[h][1], ALU.add).then_inc(S("b_a1"), 1)
                e.tensor_tensor(AC[h][2], AC[h][2], AC[h][3], ALU.add).then_inc(S("b_a3"), 1)
            drive(e, NP, 4, dense1, tail=1)

            stored_b(e)

            def gath(j, g, i):
                waitn(e, "f_m", 2 * (j - 3))
                waitn(e, "f_ix", j + 1)
                go(e)
                for k in range(4):
                    e.indirect_dma_start(out=G1[g][:, k, :], out_offset=None, in_=d_p,
                                         in_offset=bass.IndirectOffsetOnAxis(ap=idx[:, g, k:k + 1], axis=0)).then_inc(S(f"f_g{g}"), 16)
            drive(e, NG, 4, gath)

            e.wait_ge(S("f_acc"), 4 * NG)
            e.wait_ge(s_w, 16 * 16)

            def sums(j, g, i):
                waitn(e, "g_tr", j - 1)
                go(e)
                e.tensor_copy(AG[g % 2], big[:, bass.ds(2 * j, 2), :]).then_inc(S("g_ag"), 1)
                waitn(e, f"g_in{g}", 16 * uses(i, g, 0, 4))
                e.tensor_tensor(X2[g], X2[g], bc2(BB), ALU.add).then_inc(S("g_xb"), 1)
            drive(e, NP, 4, sums, tail=1)

        @block.scalar
        def _(e):
            e.wait_ge(s_pad, 3)
            for k in range(NACC):
                e.dma_start(acc[k][0:NROW, :].rearrange("(b p) c -> p b c", p=128),
                            zer.unsqueeze(1).to_broadcast([128, NT, 256])).then_inc(s_zero, 16)
            e.wait_ge(s_A, A_TID)
            for n, t in enumerate(range(TSPLIT, NT)):
                wait(e, s_Ac, n)
                e.activation(junka[0:125, :], tid_f[0:125, :], ACT.Sign, bias=thr[0:125, t:t + 1],
                             accum_out=sgn[0:125, t:t + 1]).then_inc(s_Ac, 1)

            def dense(j, g, i):
                h = g % 2
                if not done(j, NP, 2):
                    waitn(e, "d_var", j - 1)
                    e.activation(sm(g - 2, 64, 8), sm(g - 2, 56, 8), ACT.Sqrt).then_inc(S("d_sq"), 1)
                if not done(j, NP, 1):
                    waitn(e, "d_rv", j - 2)
                    waitn(e, "d_xc", j)
                    e.activation(SQ0[1 - h], XC0[1 - h], ACT.Square).then_inc(S("d_s2"), 1)
                if not done(j, NP):
                    waitn(e, "d_xc", j - 1)
                    waitn(e, "d_gm", j - 1)
                    waitn(e, "d_fc", j - 1)
                    waitn(e, "d_mm", j + 1)
                    e.activation(F0[h], q2(PS[2 + h][:, :]), ACT.Relu).then_inc(S("d_re"), 1)
                    if known(j, lambda j: j == 0):
                        e.wait_ge(s_A, A_TILE)
                    waitn(e, "d_re", j + 1)
                    go(e)
                    e.activation(big[:, bass.ds(2 * j, 2), 0:128], F0[h][:, :, 128:256], ACT.Copy).then_inc(S("d_fc"), 1)
            drive(e, NP + 2, 4, dense, tail=3)

            for n in range(3 * NC):
                e.wait_ge(s_Ap, n + 2)
                kind, cc = n // NC, n % NC
                e.activation(tab[:, cc * 32:(cc + 1) * 32, kind, :],
                             PS[n % 2][:, 0:128].rearrange("p (a b) -> p a b", b=4), ACT.Copy).then_inc(s_At, 1)

            e.wait_ge(s_zero, 16 * NACC)

            def edge0(j, g, i):
                if not done(j, NG, 1):
                    waitn(e, "e_d", j - 2)
                    waitn(e, "e_c", j)
                    e.activation(CS[(g - 1) % 2], q4(PS[2 + (g - 1) % 2][:, :]), ACT.Copy).then_inc(S("e_cc"), 1)
                if not done(j, NG, 2):
                    for k in range(4):
                        waitn(e, f"e_sc{k}", (j - 3) * 16)
                    waitn(e, "e_d", j - 1)
                    for h in range(2):
                        e.activation(DS[g % 2][:, 2 * h:2 * h + 2, :], q2(PS[4 + 2 * (g % 2) + h][:, :]), ACT.Copy)\
                         .then_inc(S("e_dc"), 1)
            drive(e, NG + 2, 4, edge0, tail=2)

            def densb(j, g, i):
                h = g % 2
                if not done(j, NP, 2):
                    waitn(e, "b_var", j - 1)
                    e.activation(sm(g - 2, 64, 8), sm(g - 2, 56, 8), ACT.Sqrt).then_inc(S("b_sq"), 1)
                if not done(j, NP, 3):
                    waitn(e, "b_v2", j - 2)
                    e.activation(sm(g - 3, 100, 2), sm(g - 3, 98, 2), ACT.Sqrt).then_inc(S("b_sr"), 1)
                if not done(j, NP, 4):
                    waitn(e, f"b_s2{h}", 16 * uses2(i, g, 6))
                    waitn(e, "b_tr", j - 3)
                    e.activation(XT1[h], q4(PS[h][:, :]), ACT.Copy).then_inc(S("b_xt"), 1)
                if not done(j, NP, 1):
                    waitn(e, "b_rv", j - 2)
                    waitn(e, "b_xc", j)
                    e.activation(SQ1[1 - h], XC1[1 - h], ACT.Square).then_inc(S("b_s2"), 1)
                if not done(j, NP, 5):
                    waitn(e, f"b_s3{1 - h}", 32 * uses2(i, g, 7))
                    waitn(e, "b_mm", j - 4)
                    for b in range(2):
                        e.activation(PQ[1 - h][:, b, :], PS[2 + 2 * (1 - h) + b][:, :], ACT.Copy).then_inc(S("b_pq"), 1)
                if not done(j, NP, 3):
                    waitn(e, f"b_s1{1 - h}", 16 * uses2(i, g, 5))
                    waitn(e, "b_tr", j - 4)
                    waitn(e, "b_rn", j - 2)
                    for b in range(2):
                        e.activation(XN[1 - h][:, b, :], X1[(g - 3) % 4][:, b, :], ACT.Identity,
                                     bias=sm(g - 3, 104 + b, 1), scale=sm(g - 3, 102 + b, 1)).then_inc(S("b_nm"), 1)
            drive(e, NP + 5, 4, densb, head=2, tail=6)
            stored_b(e)

            def window1(j, g):
                e.activation(win[:, g % 4, :, :], tab[:, j, :, :], ACT.Copy).then_inc(S("f_win"), 1)
                e.activation(idx[:, g % 4, :], tab[:, j, 1, :], ACT.Copy).then_inc(S("f_ix"), 1)
            window1(0, 0)
            window1(1, 1)

            def edge1(j, g, i):
                if not done(j + 2, NG):
                    waitn(e, f"f_g{(g + 2) % 4}", 64 * uses(i, g, 2, 4))
                    waitn(e, "f_oh", j - 1)
                    go(e)
                    window1(j + 2, g + 2)
                if not done(j, NG):
                    waitn(e, "f_qe", j - 1)
                    waitn(e, "f_tr", j + 1)
                    e.activation(OT1[g % 2], q4(PS[g % 2][:, :]), ACT.Copy).then_inc(S("f_ot"), 1)
                if not done(j, NG, 1):
                    waitn(e, "f_m", 2 * j)
                    e.activation(M1[(g - 1) % 2], M1[(g - 1) % 2], ACT.Relu).then_inc(S("f_re"), 1)
            drive(e, NG + 1, 4, edge1, tail=5)

            e.wait_ge(S("f_acc"), 4 * NG)

            def densg(j, g, i):
                h = g % 2
                if not done(j, NP, 1):
                    waitn(e, "g_mm", j - 2)
                    waitn(e, "g_tr", j)
                    e.activation(AT[1 - h], q4(PS[1 - h][:, :]), ACT.Copy).then_inc(S("g_at"), 1)
                if not done(j, NP, 2):
                    waitn(e, "g_n1", 2 * (j - 3))
                    waitn(e, "g_mm", j - 1)
                    e.activation(H2[h], q2(PS[2 + h][:, :]), ACT.Relu).then_inc(S("g_re"), 1)
                if not done(j, NP, 3):
                    waitn(e, "g_n2", 2 * (j - 4))
                    waitn(e, "g_rn", j - 2)
                    for b in range(2):
                        e.activation(N2[1 - h][:, b, :], H2[1 - h][:, b, :], ACT.Identity,
                                     bias=sm(g - 3, 104 + b, 1), scale=sm(g - 3, 102 + b, 1)).then_inc(S("g_n1"), 1)
                if not done(j, NP, 4):
                    waitn(e, f"g_st{h}", 16 * uses2(i, g, 6))
                    waitn(e, "g_rm", j - 3)
                    for b in range(2):
                        e.activation(O2[h][:, b, :], N2[h][:, b, :], ACT.Identity,
                                     bias=sm(g - 4, 54 + b, 1), scale=sm(g - 4, 52 + b, 1)).then_inc(S("g_n2"), 1)
                if not done(j, NP, 2):
                    waitn(e, "g_v1", j - 1)
                    e.activation(sm(g - 2, 100, 2), sm(g - 2, 98, 2), ACT.Sqrt).then_inc(S("g_sq"), 1)
                if not done(j, NP, 3):
                    waitn(e, "g_v2", j - 2)
                    e.activation(sm(g - 3, 50, 2), sm(g - 3, 48, 2), ACT.Sqrt).then_inc(S("g_sr"), 1)
            drive(e, NP + 4, 4, densg, head=2, tail=5)

        @block.tensor
        def _(e):
            e.wait_ge(s_pad, 3)
            e.wait_ge(s_A, A_CNT)
            e.matmul(PS[7][:, 0:100], ones[0:125, :], cnt[0:125, :], start=True, stop=True).then_inc(s_Ap, 1)
            e.wait_ge(s_const, 16)
            e.wait_ge(s_A, A_FLAG)

            def place():
                def one(j, g, i):
                    waitn(e, "u_b", j)
                    waitn(e, "u_o", j + 1)
                    e.matmul(PS[6][0:125, 0:NT], c[0:125, C_LT:C_LT + 125], fO[0:125, :], start=True, stop=True)
                    e.matmul(PS[6][:, 128:128 + NT], ones[0:125, :], fO[0:125, :], start=True, stop=True).then_inc(S("u_mm"), 1)
                drive(e, 1600, 1, one)
            unsorted(e, "pe_u", place)

            e.wait_ge(s_w, 16 * 13)
            e.wait_ge(s_A, A_BIAS)

            def bias(o, n):
                return e.matmul(o, onesb[0:3, :], b3[0:3, n, :], start=False, stop=True)

            def dense(j, g, i):
                h = g % 2
                waitn(e, "d_re", j - 1)
                waitn(e, f"d_xt{g}", 16 * uses(i, g, 0, 4))
                for b in range(2):
                    o = PS[2 + h][:, b * 256:(b + 1) * 256]
                    for k in range(2):
                        e.matmul(o, XT0[g][:, k, b * 128:(b + 1) * 128], w0[:, k, :], start=(k == 0), stop=False)
                    m = bias(o, 0)
                m.then_inc(S("d_mm"), 1)
            drive(e, NP, 4, dense, tail=1)

            e.wait_ge(s_A, A_LOC)
            for n in range(3 * NC):
                kind, cc = n // NC, n % NC
                if n >= 2:
                    e.wait_ge(s_At, n - 1)
                e.transpose(PS[n % 2][:, 0:128], (gD, gS, gW)[kind][:, cc, :], ident).then_inc(s_Ap, 1)
            e.wait_ge(s_tl, 32)
            e.wait_ge(S("d_fc"), NP)
            e.wait_ge(S("d_gm"), NP)
            regs = [e.alloc_register(f"pet{k}") for k in range(4)]

            def edge0(j, g, i):
                if not done(j, NG):
                    waitn(e, "e_s", j - 1)
                    waitn(e, "e_win", j + 1)
                    for k in range(4):
                        m = e.transpose(PS[g % 2][:, k * 128:(k + 1) * 128],
                                        win[:, g % 2, 1, k:k + 1].to_broadcast([128, 128]), ident)
                    m.then_inc(S("e_r"), 1)
                if not done(j, NG, 1):
                    waitn(e, "e_cc", j - 2)
                    waitn(e, "e_oh", j)
                    waitn(e, "e_sw", j)
                    q = (g - 1) % 2
                    for k in range(4):
                        m = e.matmul(PS[2 + q][:, k * 128:(k + 1) * 128], OH[q][:, k, :], SW[q][:, k, :], start=True, stop=True)
                    m.then_inc(S("e_c"), 1)
                if not done(j, NG, 2):
                    q = g % 2
                    e.load(regs, trow[0:1, bass.ds(j * 4 - 8, 4)])
                    ts = [e.snap(r, min_val=0, max_val=NT - 1) for r in regs]
                    waitn(e, "e_dc", 2 * (j - 3))
                    waitn(e, "e_cc", j - 1)
                    for k, t in enumerate(ts):
                        m = e.matmul(PS[4 + 2 * q + k // 2][:, (k % 2) * 256:(k % 2) * 256 + 256],
                                     CS[q][:, k, :], big[:, t, :], start=True, stop=True)
                    m.then_inc(S("e_d"), 1)
            drive(e, NG + 2, 4, edge0, tail=2)

            def densb(j, g, i):
                h = g % 2
                if not done(j, NP, 3):
                    q = 1 - h
                    waitn(e, "b_xt", j - 4)
                    waitn(e, "b_nm", 2 * (j - 2))
                    for b in range(2):
                        for k in range(2):
                            m = e.transpose(PS[q][:, (2 * b + k) * 128:(2 * b + k + 1) * 128],
                                            XN[q][:, b, k * 128:(k + 1) * 128], ident)
                    m.then_inc(S("b_tr"), 1)
                if not done(j, NP, 4):
                    waitn(e, "b_pq", 2 * (j - 5))
                    waitn(e, "b_xt", j - 3)
                    for b in range(2):
                        o = PS[2 + 2 * h + b]
                        for k in range(2):
                            e.matmul(o[:, :], XT1[h][:, 2 * b + k, :], wm[:, k, :], start=(k == 0), stop=False)
                        m = bias(o[:, 0:256], 1)
                    m.then_inc(S("b_mm"), 1)
            drive(e, NP + 4, 4, densb, head=2, tail=5)
            e.wait_ge(S("b_pq"), 2 * NP)

            def edge1(j, g, i):
                if not done(j, NG):
                    waitn(e, "f_ot", j - 1)
                    waitn(e, "f_oh", j + 1)
                    for k in range(4):
                        m = e.transpose(PS[g % 2][:, k * 128:(k + 1) * 128], OH1[g][:, k, :], ident)
                    m.then_inc(S("f_tr"), 1)
                if not done(j, NG, 3):
                    q = (g - 3) % 2
                    waitn(e, "f_acc", 4 * (j - 4))
                    waitn(e, "f_re", j - 2)
                    for k in range(4):
                        m = e.matmul(PS[4 + 2 * q + k // 2][:, (k % 2) * 256:(k % 2) * 256 + 256],
                                     OH1[(g - 3) % 4][:, k, :], M1[q][:, k, :], start=True, stop=True)
                    m.then_inc(S("f_ag"), 1)
                if not done(j, NG, 1):
                    q = (g - 1) % 2
                    waitn(e, "f_m", 2 * (j - 1))
                    waitn(e, "f_ot", j)
                    waitn(e, f"f_q{(g - 1) % 4}", 64 * uses(i, g, 1, 4))
                    for k in range(4):
                        m = e.matmul(PS[2 + k // 2][:, (k % 2) * 256:(k % 2) * 256 + 256],
                                     OT1[q][:, k, :], Q1[q][:, k, :], start=True, stop=True)
                    m.then_inc(S("f_qe"), 1)
            drive(e, NG + 3, 4, edge1, head=2, tail=3)
            e.wait_ge(s_w, 16 * 16)

            def densg(j, g, i):
                h = g % 2
                if not done(j, NP):
                    waitn(e, "g_at", j - 1)
                    waitn(e, "g_ag", j + 1)
                    for b in range(2):
                        for k in range(2):
                            m = e.transpose(PS[h][:, (2 * b + k) * 128:(2 * b + k + 1) * 128],
                                            AG[h][:, b, k * 128:(k + 1) * 128], ident)
                    m.then_inc(S("g_tr"), 1)
                if not done(j, NP, 1):
                    q = 1 - h
                    waitn(e, "g_re", j - 2)
                    waitn(e, "g_at", j)
                    waitn(e, f"g_xt{q}", 16 * uses2(i, g, 1))
                    for b in range(2):
                        o = PS[2 + q][:, b * 256:(b + 1) * 256]
                        for k in range(2):
                            e.matmul(o, XT2[q][:, 2 * b + k, :], WU[:, k, :], start=(k == 0), stop=False)
                        for k in range(2):
                            e.matmul(o, AT[q][:, 2 * b + k, :], WU[:, 2 + k, :], start=False, stop=False)
                        m = bias(o, 2)
                    m.then_inc(S("g_mm"), 1)
            drive(e, NP + 1, 4, densg, tail=2)

        @block.vector
        def _(e):
            n = [0]

            def A1(ins):
                n[0] += 1
                ins.then_inc(s_A, 1)
                e.wait_ge(s_A, n[0])

            e.wait_ge(s_const, 16)
            A1(e.tensor_scalar(thr, c[:, C_IO:C_IO + 100], -1.0, 0.5, ALU.mult, ALU.add))
            e.wait_ge(s_dl, 64)
            A1(e.tensor_scalar(sid_i[0:125, :], dst_i[0:125, :], 7, None, ALU.arith_shift_right))
            A1(e.tensor_copy(tid_f[0:125, :], sid_i[0:125, :]))
            assert n[0] == A_TID
            A1(e.tensor_copy(tid_b[0:125, :], sid_i[0:125, :]))
            A1(e.tensor_copy(dst_f[0:125, :], dst_i[0:125, :]))
            A1(e.tensor_copy(nxt_f[0:125, :], nxt_i[0:125, :]))
            A1(e.memset(cnt[:, :], 0.0))
            A1(e.tensor_tensor(junk[0:125, :], dst_f[0:125, :], nxt_f[0:125, :], ALU.is_gt))
            A1(e.tensor_reduce(cnt[0:125, 99:100], junk[0:125, :], AX.X, ALU.add))
            for t in range(1, TSPLIT):
                A1(e.tensor_scalar(junkb[0:125, :], tid_b[0:125, :], float(t), 0.0, ALU.is_lt, ALU.add,
                                   accum_out=cnt[0:125, t:t + 1]))
            A1(e.memset(cnt[0:125, NT:NT + 1], float(E // 125)))
            e.wait_ge(s_Ac, NT - TSPLIT)
            A1(e.tensor_scalar(cnt[0:125, TSPLIT:NT], sgn[0:125, TSPLIT:NT], -0.5, 800.0, ALU.mult, ALU.add))
            assert n[0] == A_CNT
            e.wait_ge(s_Ap, 1)
            A1(e.tensor_copy(st, PS[7][:, 0:100]))
            A1(e.tensor_copy(st_i, st))
            assert n[0] == A_FLAG

            def place():
                e.tensor_copy(fB, st[:, 0:NT]).then_inc(S("u_b0"), 1)
                e.wait_ge(S("u_b0"), 1)
                e.wait_ge(S("u_l"), 32)

                def one(j, g, i):
                    e.tensor_copy(fcol[0:125, :], tid_f[0:125, bass.ds(j, 1)]).then_inc(S("u_c"), 1)
                    waitn(e, "u_c", j + 1)
                    e.tensor_scalar(fO[0:125, :], c[0:125, C_IO:C_IO + NT], fcol[0:125, :], None, ALU.is_equal).then_inc(S("u_o"), 1)
                    for k in range(3):
                        waitn(e, f"u_sc{k}", j * 16)
                    go(e)
                    e.tensor_copy(fval[0:125, 0:1].bitcast(i32), dst_i[0:125, bass.ds(j, 1)])
                    e.tensor_copy(fval[0:125, 1:2], fsrc[0:125, bass.ds(j, 1)])
                    e.tensor_copy(fval[0:125, 2:3], few[0:125, bass.ds(j, 1)]).then_inc(S("u_v"), 1)
                    waitn(e, "u_mm", j + 1)
                    e.tensor_tensor(fR[0:125, :], PS[6][0:125, 0:NT], fB[0:125, :], ALU.add).then_inc(S("u_r"), 1)
                    waitn(e, "u_r", j + 1)
                    e.tensor_tensor(fM[0:125, :], fR[0:125, :], fO[0:125, :], ALU.mult).then_inc(S("u_p"), 1)
                    e.tensor_tensor(fB, fB, PS[6][:, 128:128 + NT], ALU.add).then_inc(S("u_b"), 1)
                    waitn(e, "u_p", j + 1)
                    e.tensor_reduce(fpos[0:125, :], fM[0:125, :], AX.X, ALU.add).then_inc(S("u_q"), 1)
                    waitn(e, "u_q", j + 1)
                    e.tensor_copy(fpi[0:125, :], fpos[0:125, :]).then_inc(S("u_pi"), 1)
                    waitn(e, "u_pi", j + 1)
                    waitn(e, "u_b", j + 1)
                    go(e)
                drive(e, 1600, 1, one)
            unsorted(e, "dve_u", place)

            A1(e.tensor_scalar(fi_i, st_i, 7, None, ALU.arith_shift_right))
            A1(e.tensor_scalar(bA, st, 127.0, None, ALU.add))
            A1(e.tensor_copy(la_i, bA))
            A1(e.tensor_scalar(le_i, la_i, 7, None, ALU.arith_shift_right))
            A1(e.tensor_copy(fi, fi_i))
            A1(e.tensor_copy(la, le_i))
            A1(e.tensor_tensor(ne[:, 0:NT], st[:, 1:NT + 1], st[:, 0:NT], ALU.is_gt))
            A1(e.tensor_tensor(dC[:, 0:NT], la[:, 1:NT + 1], fi[:, 0:NT], ALU.subtract))
            A1(e.memset(bA, 0.0))
            A1(e.tensor_tensor(bA[:, 1:NT], dC[:, 0:NT - 1], ne[:, 0:NT - 1], ALU.mult))
            a, b = bA, bB
            for k in range(7):
                d = 1 << k
                A1(e.tensor_copy(b[:, 0:d], a[:, 0:d]))
                A1(e.tensor_tensor(b[:, d:NT], a[:, d:NT], a[:, 0:NT - d], ALU.add))
                a, b = b, a
            A1(e.tensor_tensor(la[:, 0:NT], fi[:, 0:NT], a[:, 0:NT], ALU.subtract))
            A1(e.tensor_tensor(dC[:, 1:NT], la[:, 1:NT], la[:, 0:NT - 1], ALU.subtract))
            for cc in range(NC):
                s = c[:, C_STEP + cc:C_STEP + cc + 1]
                A1(e.tensor_scalar(gj[:, 1:NT], a[:, 1:NT], s, 0.0, ALU.is_le, ALU.add, accum_out=tS[:, cc:cc + 1]))
                A1(e.tensor_tensor(gj2[:, 1:NT], gj[:, 1:NT], dC[:, 1:NT], ALU.mult))
                A1(e.tensor_reduce(cS[:, cc:cc + 1], gj2[:, 1:NT], AX.X, ALU.add))
            A1(e.tensor_copy(tI, tS))
            A1(e.tensor_tensor(tfl, cS, c[:, C_STEP:C_STEP + NC], ALU.add))
            A1(e.tensor_scalar(cS, tfl, float(CH), None, ALU.min))
            A1(e.tensor_copy(cI, cS))
            assert n[0] == A_CHUNK
            A1(e.tensor_scalar(tfl, tS, 128.0, None, ALU.mult))
            e.wait_ge(s_w, 16 * 13)
            A1(e.memset(onesb[:, :], 1.0))
            A1(e.memset(bsum[0:3], 0.0))
            for k in range(3):
                A1(e.tensor_copy(bbf[0:3], brow[0:3]))
                A1(e.tensor_copy(bpart[0:3], bbf[0:3]))
                A1(e.tensor_tensor(brow[0:3], brow[0:3], bpart[0:3], ALU.subtract))
                A1(e.tensor_scalar(brem[0:3], bpart[0:3], c[0:3, C_ID + k:C_ID + k + 1], None, ALU.mult))
                A1(e.tensor_tensor(bsum[0:3], bsum[0:3], brem[0:3], ALU.add))
            A1(e.tensor_copy(b3[:, :, :], bsum[0:3]))
            assert n[0] == A_BIAS

            def dense(j, g, i):
                h = g % 2
                p1, p2, p3 = (not done(j, NP, k) for k in (1, 2, 3))
                if not done(j, NP):
                    waitn(e, "d_ar", j)
                    waitn(e, "d_re", j + 1)
                    e.tensor_tensor(U0, F0[h], bc2(attb[:, :]), ALU.mult).then_inc(S("d_u"), 1)
                if p1:
                    waitn(e, "d_s2", j)
                    e.tensor_reduce(bh(sm(g - 1, 48, 8)), h4(SQ0[1 - h]), AX.X, ALU.add).then_inc(S("d_rv"), 1)
                if not done(j, NP):
                    waitn(e, "d_u", j + 1)
                    e.tensor_reduce(bh(sm(g, 0, 16)), U0.rearrange("p b (h d) -> p b h d", h=8), AX.X, ALU.add).then_inc(S("d_ar"), 1)
                if p1:
                    waitn(e, "d_rv", j)
                    e.tensor_scalar(sm(g - 1, 56, 8), sm(g - 1, 48, 8), 1.0 / 32, 1e-9, ALU.mult, ALU.add).then_inc(S("d_var"), 1)
                if not done(j, NP):
                    e.tensor_reduce(bh(sm(g, 32, 8)), h4(F0[h][:, :, 0:128]), AX.X, ALU.add).then_inc(S("d_hs"), 1)
                if p2:
                    waitn(e, "d_sq", j - 1)
                    e.reciprocal(sm(g - 2, 72, 8), sm(g - 2, 64, 8)).then_inc(S("d_rc"), 1)
                if not done(j, NP):
                    waitn(e, "d_gm", j - 3)
                    waitn(e, "d_ar", j + 1)
                    e.scalar_tensor_tensor(sm(g, 16, 16), sm(g, 0, 16), 0.2, sm(g, 0, 16), ALU.mult, ALU.max).then_inc(S("d_lk"), 1)
                    waitn(e, "d_hs", j + 1)
                    e.tensor_scalar(sm(g, 40, 8), sm(g, 32, 8), 1.0 / 32, None, ALU.mult).then_inc(S("d_me"), 1)
                if p2:
                    waitn(e, "d_sc", j - 3)
                    waitn(e, "d_rc", j - 1)
                    e.tensor_tensor(h4(Z0[h]), h4(XC0[h]), bh(sm(g - 2, 72, 8)).unsqueeze(3).to_broadcast(hb), ALU.mult)\
                     .then_inc(S("d_z"), 1)
                if not done(j, NP):
                    waitn(e, "d_lk", j + 1)
                    go(e)
                    e.tensor_copy(ats[:, bass.ds(2 * j, 2), :],
                                  sm(g, 16, 16).rearrange("p (b o h) -> p b o h", b=2, o=2)[:, :, 0, :]).then_inc(S("d_as"), 1)
                if p3:
                    q = 1 - h
                    waitn(e, "d_xo", j - 2)
                    waitn(e, "d_sc", j - 2)
                    x0 = X0[(g - 3) % 4][:, :, 0:128]
                    e.tensor_tensor(x0, x0, Y0[q], ALU.add).then_inc(S("d_x"), 1)
                if not done(j, NP):
                    waitn(e, "d_z", j - 1)
                    waitn(e, "d_me", j + 1)
                    e.tensor_tensor(h4(XC0[h]), h4(F0[h][:, :, 0:128]), bh(sm(g, 40, 8)).unsqueeze(3).to_broadcast(hb), ALU.subtract)\
                     .then_inc(S("d_xc"), 1)
            drive(e, NP + 3, 4, dense, tail=4)

            e.wait_ge(s_Ag, 16 * 3 * NC)
            A1(e.tensor_copy(gS, gS.bitcast(i32)))
            A1(e.tensor_tensor(gD, gD.bitcast(i32), tfl.unsqueeze(2).to_broadcast([128, NC, 128]), ALU.subtract))
            assert n[0] == A_LOC
            e.wait_ge(s_At, 3 * NC)
            e.tensor_scalar(tab[:, :, 3, :], tab[:, :, 1, :], c[:, C_DUMP:C_DUMP + 1], -1.0, ALU.subtract, ALU.mult).then_inc(s_At, 1)
            e.wait_ge(s_At, 3 * NC + 1)
            for g in range(4):
                e.wait_ge(S(f"d_st{g}"), 16 * (13 if g == 0 else 12))

            def window(j, g):
                e.tensor_copy(win[:, g % 2, :, :], tab[:, j, :, :]).then_inc(S("e_win"), 1)

            window(0, 0)

            def edge0(j, g, i):
                q = g % 2
                waitn(e, "e_c", j - 1)
                waitn(e, "e_win", j + 1)
                e.tensor_tensor(OH[q], iota.unsqueeze(1).to_broadcast(b4),
                                win[:, q, 0, :].unsqueeze(2).to_broadcast(b4), ALU.is_equal).then_inc(S("e_oh"), 1)
                waitn(e, "e_r", j + 1)
                e.tensor_tensor(SS, q4(PS[q][:, :]), win[:, q, 1, :].unsqueeze(2).to_broadcast(b4), ALU.is_equal).then_inc(S("e_s"), 1)
                if not done(j + 1, NG):
                    waitn(e, "e_ix", j)
                    go(e)
                    window(j + 1, g + 1)
                waitn(e, "e_s", j + 1)
                e.tensor_tensor(TT, SS, ltri.unsqueeze(1).to_broadcast(b4), ALU.mult).then_inc(S("e_tt"), 1)
                e.tensor_tensor(SW[q], SS, win[:, q, 2, :].unsqueeze(2).to_broadcast(b4), ALU.mult).then_inc(S("e_sw"), 1)
                waitn(e, "e_tt", j + 1)
                ct = sm(0, 96, 4)
                e.tensor_reduce(ct, TT, AX.X, ALU.add).then_inc(S("e_ct"), 1)
                waitn(e, "e_ct", j + 1)
                e.scalar_tensor_tensor(sm(0, 100, 4), ct, 0.5, win[:, q, 3, :], ALU.is_gt, ALU.mult).then_inc(S("e_fl"), 1)
                waitn(e, "e_fl", j + 1)
                for k in range(4):
                    waitn(e, f"e_sc{k}", (j - 3) * 16)
                e.tensor_tensor(idx[:, g, :], sm(0, 100, 4), win[:, q, 1, :], ALU.add).then_inc(S("e_ix"), 1)
            drive(e, NG, 4, edge0, tail=1)
            for k in range(4):
                e.wait_ge(S(f"e_sc{k}"), 16 * NG)

            def densb(j, g, i):
                h = g % 2
                p0, p1, p2, p3 = (not done(j, NP, k) for k in (0, 1, 2, 3))
                if p0:
                    waitn(e, "b_y", j)
                    waitn(e, "b_v", j)
                    waitn(e, "b_a1", j + 1)
                    waitn(e, "b_a3", j + 1)
                    e.tensor_tensor(SA, AC[h][0], AC[h][2], ALU.add).then_inc(S("b_a"), 1)
                if p1:
                    waitn(e, "b_s2", j)
                    e.tensor_reduce(bh(sm(g - 1, 48, 8)), h4(SQ1[1 - h]), AX.X, ALU.add).then_inc(S("b_rv"), 1)
                if p0:
                    waitn(e, "b_a", j + 1)
                    go(e)
                    e.tensor_tensor(h4(YB), h4(SA[:, :, 0:128]), ats[:, bass.ds(2 * j, 2), :].unsqueeze(3).to_broadcast(hb), ALU.mult)\
                     .then_inc(S("b_y"), 1)
                if p1:
                    waitn(e, "b_rv", j)
                    e.tensor_scalar(sm(g - 1, 56, 8), sm(g - 1, 48, 8), 1.0 / 32, 1e-9, ALU.mult, ALU.add).then_inc(S("b_var"), 1)
                if p2:
                    waitn(e, "b_sq", j - 1)
                    e.reciprocal(sm(g - 2, 72, 8), sm(g - 2, 64, 8)).then_inc(S("b_rc"), 1)
                if p0:
                    waitn(e, "b_xc", j)
                    waitn(e, "b_y", j + 1)
                    e.tensor_tensor(VV, YB, SA[:, :, 128:256], ALU.add).then_inc(S("b_v"), 1)
                if p2:
                    waitn(e, "b_rc", j - 1)
                    e.tensor_tensor(h4(Z1), h4(XC1[h]), bh(sm(g - 2, 72, 8)).unsqueeze(3).to_broadcast(hb), ALU.mult)\
                     .then_inc(S("b_z"), 1)
                if p0:
                    waitn(e, "b_v", j + 1)
                    e.tensor_reduce(bh(sm(g, 32, 8)), h4(VV), AX.X, ALU.add).then_inc(S("b_hs"), 1)
                if p2:
                    waitn(e, "b_z", j - 1)
                    e.tensor_tensor(Z2, Z1, bc2(scb[:, 128:256]), ALU.mult).then_inc(S("b_sc"), 1)
                if p0:
                    waitn(e, "b_hs", j + 1)
                    e.tensor_scalar(sm(g, 40, 8), sm(g, 32, 8), 1.0 / 32, None, ALU.mult).then_inc(S("b_me"), 1)
                if p2:
                    waitn(e, f"b_in{(g - 2) % 4}", 16 * uses(i, g, 2, 4))
                    waitn(e, "b_sc", j - 1)
                    x1 = X1[(g - 2) % 4]
                    e.tensor_tensor(x1[:, :, 128:256], x1[:, :, 128:256], Z2, ALU.add).then_inc(S("b_x"), 1)
                if p3:
                    waitn(e, "b_sr", j - 2)
                    e.reciprocal(sm(g - 3, 102, 2), sm(g - 3, 100, 2)).then_inc(S("b_r2"), 1)
                if p0:
                    waitn(e, "b_me", j + 1)
                    e.tensor_tensor(h4(XC1[h]), h4(VV), bh(sm(g, 40, 8)).unsqueeze(3).to_broadcast(hb), ALU.subtract)\
                     .then_inc(S("b_xc"), 1)
                if p2:
                    waitn(e, "b_x", j - 1)
                    for b in range(2):
                        e.bn_stats(sm(g - 2, 80 + 6 * b, 6), x1[:, b, :]).then_inc(S("b_bn"), 1)
                if p3:
                    waitn(e, "b_r2", j - 2)
                    e.scalar_tensor_tensor(sm(g - 3, 104, 2), sm(g - 3, 92, 4).rearrange("p (b t) -> p b t", t=2)[:, :, 0], -1.0,
                                           sm(g - 3, 102, 2), ALU.mult, ALU.mult).then_inc(S("b_rn"), 1)
                if p2:
                    waitn(e, "b_bn", 2 * (j - 1))
                    go(e)
                    for b in range(2):
                        e.bn_aggr(sm(g - 2, 92 + 2 * b, 2), sm(g - 2, 80 + 6 * b, 6)).then_inc(S("b_ag"), 1)
                    waitn(e, "b_ag", 2 * (j - 1))
                    e.tensor_scalar(sm(g - 2, 98, 2), sm(g - 2, 92, 4).rearrange("p (b t) -> p b t", t=2)[:, :, 1], 1e-5, None, ALU.add)\
                     .then_inc(S("b_v2"), 1)
            drive(e, NP + 3, 4, densb, tail=4)

            stored_b(e)
            for k in range(NT // 7):
                e.memset(big[:, 7 * k:7 * k + 7, :], 0.0).then_inc(S("f_z"), 1)
            e.wait_ge(S("f_z"), NT // 7)
            regs = [e.alloc_register(f"dvt{k}") for k in range(4)]

            def onehot(j, g):
                waitn(e, "f_ag", j - 3)
                waitn(e, "f_win", j + 1)
                e.tensor_tensor(OH1[g % 4], iota.unsqueeze(1).to_broadcast(b4),
                                win[:, g % 4, 0, :].unsqueeze(2).to_broadcast(b4), ALU.is_equal).then_inc(S("f_oh"), 1)
            onehot(0, 0)

            def edge1(j, g, i):
                p1, p4 = not done(j, NG, 1), not done(j, NG, 4)
                if p4:
                    e.load(regs, trow[0:1, bass.ds(j * 4 - 16, 4)])
                    ts = [e.snap(r, min_val=0, max_val=NT - 1) for r in regs]
                    waitn(e, "f_ag", j - 3)
                q = (g - 4) % 2

                def add(k):
                    if p4:
                        waitn(e, "f_acc", (j - 4) * 4 + k)
                        e.tensor_tensor(big[:, ts[k], :], big[:, ts[k], :],
                                        PS[4 + 2 * q + k // 2][:, (k % 2) * 256:(k % 2) * 256 + 256], ALU.add).then_inc(S("f_acc"), 1)

                def message(h):
                    if p1:
                        p = (g - 1) % 2
                        if h == 0:
                            waitn(e, "f_ag", j - 2)
                            waitn(e, "f_qe", j)
                            waitn(e, f"f_g{(g - 1) % 4}", 64 * uses(i, g, 1, 4))
                        e.tensor_tensor(M1[p][:, 2 * h:2 * h + 2, :], G1[(g - 1) % 4][:, 2 * h:2 * h + 2, :],
                                        q2(PS[2 + h][:, :]), ALU.add).then_inc(S("f_m"), 1)
                for k in range(4):
                    add(k)
                if not done(j + 1, NG):
                    onehot(j + 1, g + 1)
                message(0)
                message(1)
            drive(e, NG + 4, 4, edge1, head=2, tail=8)

            e.wait_ge(S("f_acc"), 4 * NG)
            e.wait_ge(s_w, 16 * 16)

            def densg(j, g, i):
                h = g % 2
                p2, p3 = not done(j, NP, 2), not done(j, NP, 3)

                def stats(p, lag, buf, base, name):
                    if p:
                        for b in range(2):
                            e.bn_stats(sm(g - lag, base + 6 * b, 6), buf[:, b, :]).then_inc(S(name), 1)

                def aggr(p, lag, base, to, name, src_name):
                    if p:
                        waitn(e, src_name, 2 * (j - lag + 1))
                        go(e)
                        for b in range(2):
                            e.bn_aggr(sm(g - lag, to + 2 * b, 2), sm(g - lag, base + 6 * b, 6)).then_inc(S(name), 1)

                def var(p, lag, mv, to, name, src_name):
                    if p:
                        waitn(e, src_name, 2 * (j - lag + 1))
                        e.tensor_scalar(sm(g - lag, to, 2), sm(g - lag, mv, 4).rearrange("p (b t) -> p b t", t=2)[:, :, 1], 1e-5, None,
                                        ALU.add).then_inc(S(name), 1)

                def factors(p, lag, mv, sq, rc, rn, names):
                    if p:
                        waitn(e, names[0], j - lag + 1)
                        e.reciprocal(sm(g - lag, rc, 2), sm(g - lag, sq, 2)).then_inc(S(names[1]), 1)
                        waitn(e, names[1], j - lag + 1)
                        e.scalar_tensor_tensor(sm(g - lag, rn, 2), sm(g - lag, mv, 4).rearrange("p (b t) -> p b t", t=2)[:, :, 0], -1.0,
                                               sm(g - lag, rc, 2), ALU.mult, ALU.mult).then_inc(S(names[2]), 1)
                if p2:
                    waitn(e, "g_re", j - 1)
                stats(p2, 2, H2[h], 80, "g_b1")
                if p3:
                    waitn(e, "g_n1", 2 * (j - 2))
                    n2 = N2[1 - h]
                    e.tensor_tensor(n2, n2, bc2(GB), ALU.mult).then_inc(S("g_gm"), 1)
                aggr(p2, 2, 80, 92, "g_a1", "g_b1")
                if p3:
                    waitn(e, "g_xb", j - 2)
                    waitn(e, "g_gm", j - 2)
                    e.tensor_tensor(n2, n2, X2[(g - 3) % 4], ALU.add).then_inc(S("g_add"), 1)
                var(p2, 2, 92, 98, "g_v1", "g_a1")
                if p3:
                    waitn(e, "g_add", j - 2)
                stats(p3, 3, N2[1 - h], 0, "g_b2")
                factors(p2, 2, 92, 100, 102, 104, ("g_sq", "g_r1", "g_rn"))
                aggr(p3, 3, 0, 12, "g_a2", "g_b2")
                var(p3, 3, 12, 48, "g_v2", "g_a2")
                factors(p3, 3, 12, 50, 52, 54, ("g_sr", "g_r2", "g_rm"))
            drive(e, NP + 3, 4, densg, tail=4)


TSPLIT = 62
AW = 14400
A_TID = 3
A_CNT = A_TID + 6 + (TSPLIT - 1) + 2
A_FLAG = A_CNT + 2
A_TILE = A_FLAG + 10 + 14 + 2 + 3 * NC + 1
A_CHUNK = A_TILE + 3
A_BIAS = A_CHUNK + 1 + 2 + 15 + 1
A_LOC = A_BIAS + 2

_INS = ['x', 'xT', 'src', 'dst', 'edge_weight', 'L0_gnn_W', 'L0_gnn_b', 'L0_gnn_att', 'L0_gnn_scale', 'L0_gnn_offset',
        'L1_gnn_W_msg', 'L1_gnn_b_msg', 'L1_gnn_W_upd', 'L1_gnn_b_upd', 'L1_gnn_gamma', 'L1_gnn_beta']


def constants():
    import numpy as np
    c = np.zeros((128, CW), np.float32)
    p = np.arange(128, dtype=np.float32)
    c[:, C_ID:C_ID + 128] = np.eye(128)
    c[:, C_IO:C_IO + 128] = p[None, :]
    c[:, C_LT:C_LT + 128] = p[None, :] < p[:, None]
    c[:, C_PID] = p
    c[:, C_STEP:C_STEP + NC] = p[:, None] + 128 * np.arange(NC, dtype=np.float32)[None, :]
    c[:, C_DUMP] = NROW + p
    return c


def kernel(**inputs):
    import numpy as _np
    import concourse.bacc as _bacc
    from concourse import mybir as _mybir
    from concourse.bass_utils import run_bass_kernel_spmd as _run

    nc = _bacc.Bacc("TRN2", target_bir_lowering=False, num_devices=1)
    arrays, args = {}, []
    for name in _INS:
        a = _np.ascontiguousarray(inputs["x"].T if name == "xT" else inputs[name])
        arrays[f"in_{name}_dram"] = a
        args.append(nc.dram_tensor(f"in_{name}_dram", a.shape, _mybir.dt.from_np(a.dtype), kind="ExternalInput").ap())
    a = constants()
    arrays["in_cst_dram"] = a
    args.append(nc.dram_tensor("in_cst_dram", a.shape, _mybir.dt.from_np(a.dtype), kind="ExternalInput").ap())
    args.append(nc.dram_tensor("out_0_dram", (N, 256), f32, kind="ExternalOutput").ap())
    gnn(nc, *args)
    r = _run(nc, [arrays], core_ids=[0])
    return r.results[0]["out_0_dram"]
```

```python
import concourse.bass as bass
from concourse import mybir
from contextlib import ExitStack

f32 = mybir.dt.float32
i32 = mybir.dt.int32
bf16 = mybir.dt.bfloat16
ALU = mybir.AluOpType
ACT = mybir.ActivationFunctionType
AX = mybir.AxisListType

N = 12500
E = 200000
NT = 98
NP = 49
LASTR = N - 97 * 128
NROW = NT * 128
CH = 1563
CROWS = 1664
NS = 1664
NG = NS // 4
NC = 13
NAC = 32
NACC = 4
C_ID, C_IO, C_LT, C_PID, C_STEP, C_DUMP = 0, 128, 256, 384, 385, 398
CW = 399


TABS = [(kind, c0, min(c0 + 4, NC)) for kind in range(3) for c0 in range(0, NC, 4)]

SHARED = {"b_" + n: ("d_" + n, NP) for n in ("hs", "me", "mm", "rc", "rv", "s2", "sc", "sq", "var", "x", "xc", "z")}
SHARED.update({"d_xt" + g: ("a_xt" + g, 16 * (13 if g == "0" else 12)) for g in "0123"})
SHARED.update({"g_" + n: ("d_" + m, NP) for n, m in (("re", "re"), ("at", "lk"), ("tr", "u"))})
SHARED.update({"g_" + n: ("a_" + m, NP) for n, m in (("gm", "gm"), ("ag", "re"), ("xb", "lk"))})
SHARED.update({"g_" + n: ("d_" + m, 2 * NP) for n, m in (("mm", "mm"), ("sq", "sq"), ("add", "x"), ("r1", "rc"), ("v1", "var"))})
SHARED.update({"g_" + n: ("b_" + n, NP) for n in ("rn", "sr", "r2", "v2")})
SHARED.update({"g_" + n: ("b_" + m, 2 * NP) for n, m in (("n1", "nm"), ("b1", "bn"), ("a1", "ag"))})


def wait(e, sem, v):
    if isinstance(v, int):
        if v > 0:
            e.wait_ge(sem, v)
    else:
        e.wait_ge(sem, v)


def drive(e, total, u, body, head=1, tail=0):
    mid = (total - tail) // u
    for j in range(head * u):
        body(j, j % u, j // u)
    with e.Fori(head, mid) as i:
        for g in range(u):
            body(i * u + g, g, i)
    for j in range(mid * u, total):
        body(j, j % u, j // u)


def merged(part, edge):
    def body(j, g, i):
        p = part(j, g, i)
        for q in range(8):
            edge(j * 8 + q, q % 4, None)
            for f in p[q]:
                f()
    return body


def uses(i, g, d, u):
    return i + ((g - d) // u + 1)


def gate(e, s):
    e.sem_inc(s, 1)


def uses2(i, g, d):
    return i * 2 + ((g - d) // 2 + 1)


def known(j, *conditions):
    return isinstance(j, int) and any(f(j) for f in conditions)


def gnn(nc, x, xT, src, dst, ew, W0, b0, att, scale, offset, Wm, bm, Wu, bu, gam, bet, cst, out):
    ctx = ExitStack()
    with ctx:
        def sb(name, shape, dt=f32):
            return ctx.enter_context(nc.sbuf_tensor(name, shape, dt))

        sems = {}

        def S(name):
            name = SHARED[name][0] if name in SHARED else name
            if name not in sems:
                sems[name] = ctx.enter_context(nc.semaphore("q_" + name))
            return sems[name]

        def base(name):
            return SHARED[name][1] if name in SHARED else 0

        def waitn(e, name, v):
            if not isinstance(v, int) or v > 0:
                e.wait_ge(S(name), v + base(name))
                if e is nc.sync and not isinstance(v, int):
                    go(e)

        def dram(name, shape, dt=f32):
            return nc.dram_tensor(name, shape, dt).ap()

        srcT = dram("d_src", (CROWS, 128), i32)
        dstT = dram("d_dst", (CROWS, 128), i32)
        ewT = dram("d_ew", (CROWS, 128))
        d_tile = dram("d_tile", (NC, 128), i32)
        acc = [dram(f"d_acc{k}", (NROW + 128, 256)) for k in range(NACC)]
        d_xp = dram("d_xp", (NROW, 256))
        d_x1 = dram("d_x1", (NROW, 256))
        d_p = dram("d_p", (NROW, 256))
        d_q = dram("d_q", (NROW, 256))

        big = sb("big", [128, NT, 256])
        tab = sb("tab", [128, NG, 4, 4])
        c = sb("cstb", [128, CW])
        ats = sb("ats", [128, NT, 4])
        trow = sb("trow", [1, NS], i32)
        ident = c[:, C_ID:C_ID + 128]
        iota = c[:, C_IO:C_IO + 128]
        ltri = c[:, C_LT:C_LT + 128]
        ones = sb("ones", [128, 128])
        onesb = sb("onesb", [3, 128], bf16)
        b3 = sb("b3", [3, 3, 256], bf16)
        w0 = sb("w0", [128, 2, 256])
        attb = sb("attb", [128, 256])
        scb = sb("scb", [128, 256])
        ofb = sb("ofb", [128, 256])
        A = sb("arena", [128, AW])
        win = sb("win", [128, 4, 4, 4])
        idx = sb("idx", [128, 4, 4], i32)
        small = sb("small", [128, 4, 112])
        wm = sb("wm", [128, 2, 512])

        def carve(buf, start=0):
            at = [start]

            def take(*shape):
                n = 1
                for s in shape:
                    n *= s
                v = buf[:, at[0]:at[0] + n]
                at[0] += n
                assert at[0] <= buf.shape[1], at[0]
                if len(shape) == 1:
                    return v
                names = "abcd"[:len(shape)]
                return v.rearrange(f"p ({' '.join(names)}) -> p {' '.join(names)}",
                                   **{k: s for k, s in zip(names, shape)})
            return take

        PS = [ctx.enter_context(nc.psum_tensor(f"ps{i}", [128, 512], f32)) for i in range(8)]

        s_const, s_w, s_pad, s_tab, s_dl = (S(n) for n in ("const", "w", "pad", "tab", "dl"))
        s_A = S("A")
        s_Ap, s_At, s_tl = (S(n) for n in ("Ap", "At", "tl"))
        s_gate = {q.engine: S(f"gate{n}") for n, q in enumerate((nc.gpsimd, nc.vector, nc.scalar, nc.sync))}

        def go(e):
            gate(e, s_gate[e.engine])

        def q4(ap):
            return ap.rearrange("p (a b) -> p a b", a=4)

        take = carve(big[:, :, :].rearrange("p a b -> p (a b)"))
        dst_i = take(1600).bitcast(i32)
        nxt_i = take(1600).bitcast(i32)
        row_i = take(1600).bitcast(i32)
        junk = take(1600)
        sid_i = take(1600).bitcast(i32)
        tid_f = take(1600)
        junk2 = take(1600)
        fsrc = take(1600)
        few = take(1600)
        fO, fR, fM, fB = take(NT), take(NT), take(NT), take(NT)
        fcol, fpos = take(1), take(1)
        fpi = take(1).bitcast(i32)
        fval = take(3)
        brow = take(3, 256)
        bpart = take(3, 256)
        brem = take(3, 256)
        bsum = take(3, 256)
        bbf = take(3, 128).bitcast(bf16)
        gS = take(NC, 128)
        gD = take(NC, 128)
        gW = take(NC, 128)
        g13, h13 = (v[:, 0:NC * NT].rearrange("p (a b) -> p a b", a=NC) for v in (junk, junk2))
        take = carve(A)
        zer = take(256)
        padi = take(128).bitcast(i32)
        cnt = take(100)
        before = take(100)
        diag = take(100)
        thr, first, rows, part, lower, flag = (take(1) for _ in range(6))
        ri = take(1).bitcast(i32)
        st, fi, la, ne, bA, bB, dC = (take(100) for _ in range(7))
        st_i, fi_i, la_i, le_i = (take(100).bitcast(i32) for _ in range(4))
        tS, cS, tfl = (take(NC) for _ in range(3))
        cI, tI = (take(NC).bitcast(i32) for _ in range(2))
        X0 = [take(2, 256) for _ in range(4)]
        F0 = [take(2, 256) for _ in range(2)]
        U0 = take(2, 256)
        XC0 = [take(2, 128) for _ in range(2)]
        SQ0 = [take(2, 128) for _ in range(2)]
        Z0 = [take(2, 128) for _ in range(2)]
        Y0 = [take(2, 128) for _ in range(2)]
        XT0 = [take(2, 256) for _ in range(4)]
        FN = [take(2, 128) for _ in range(2)]
        UN = take(2, 128)
        take = carve(A)
        OH = [take(4, 128) for _ in range(2)]
        SS = take(4, 128)
        SW = [take(4, 128) for _ in range(2)]
        TT = take(4, 128)
        CS = [take(4, 128) for _ in range(2)]
        DS = [take(4, 256) for _ in range(2)]
        XT0B = [take(2, 256) for _ in range(4)]
        X0 = [take(2, 256) for _ in range(4)]
        FS = [take(2, 128) for _ in range(2)]
        US = take(2, 128)
        XC0 = [take(2, 128) for _ in range(2)]
        SQ0 = [take(2, 128) for _ in range(2)]
        Z0 = take(2, 128)
        Y0 = take(2, 128)
        take = carve(A)
        X1 = [take(2, 256) for _ in range(4)]
        XN = [take(2, 256) for _ in range(2)]
        XT1 = [take(4, 128) for _ in range(2)]
        PQ = [take(2, 512) for _ in range(2)]
        SA = take(2, 256)
        YB = take(2, 128)
        VV = take(2, 128)
        XC1 = [take(2, 128) for _ in range(2)]
        SQ1 = [take(2, 128) for _ in range(2)]
        Z1 = take(2, 128)
        Z2 = take(2, 128)
        take = carve(big[:, 0:NAC, :].rearrange("p a b -> p (a b)"))
        AC = [[take(2, 256) for _ in range(4)] for _ in range(4)]
        ZN = (NT - NAC) * 256 // 48
        ZB = A[:, AW - ZN:AW]
        take = carve(A)
        OH1 = [take(4, 128) for _ in range(4)]
        OT1 = [take(4, 128) for _ in range(2)]
        G1 = [take(4, 256) for _ in range(4)]
        Q1 = [take(4, 256) for _ in range(2)]
        M1 = [take(4, 256) for _ in range(2)]
        X2 = [take(2, 256) for _ in range(4)]
        take = carve(A)
        XB = [take(2, 256) for _ in range(4)]
        XT2 = [take(4, 128) for _ in range(2)]
        AG = [take(2, 256) for _ in range(2)]
        AT = [take(4, 128) for _ in range(2)]
        H2 = [take(2, 256) for _ in range(2)]
        N2 = [take(2, 256) for _ in range(2)]
        O2 = [take(2, 256) for _ in range(2)]
        WU = q4(wm[:, :, :].rearrange("p a b -> p (a b)"))
        GB, BB = attb[:, :], scb[:, :]

        def pair(t, j):
            return t[bass.ds(j * 256, 256), :].rearrange("(b p) c -> p b c", p=128)

        def sm(g, a, n):
            return small[:, g % 4, a:a + n]

        def bc2(ap):
            return ap.unsqueeze(1).to_broadcast([128, 2, ap.shape[1]])

        hb = [128, 2, 4, 32]
        b4 = [128, 4, 128]

        def h4(ap):
            return ap.rearrange("p b (h d) -> p b h d", h=4)

        def bh(ap):
            return ap.rearrange("p (b h) -> p b h", b=2)

        def q2(ap):
            return ap.rearrange("p (a b) -> p a b", a=2)

        def done(j, last, lag=0):
            return isinstance(j, int) and not 0 <= j - lag < last

        block = ctx.enter_context(nc.Block())

        def stored_b(e):
            for h, n in ((0, 25), (1, 24)):
                e.wait_ge(S(f"b_s1{h}"), 16 * n)
                e.wait_ge(S(f"b_s3{h}"), 32 * n)

        def zeroed(e):
            e.wait_ge(S("zero0"), 16 * 7)
            e.wait_ge(S("zero1"), 16 * 7)
            e.wait_ge(S("zero2"), 32 * NP)

        def unsorted(e, name, body):
            r = e.alloc_register(name)
            e.load([r], st_i[0:1, 99:100])
            with e.If_ne(r, 0):
                body()

        @block.sync
        def _(e):
            e.dma_start(dst_i[0:125, :], dst.rearrange("(p c) -> p c", p=125)).then_inc(s_dl, 16)
            e.dma_start(nxt_i[0:124, :], dst[1:1 + 124 * 1600].rearrange("(p c) -> p c", p=124)).then_inc(s_dl, 16)
            e.dma_start(nxt_i[124:125, 0:1599], dst[1 + 124 * 1600:E].rearrange("(a c) -> a c", a=1)).then_inc(s_dl, 16)
            e.dma_start(nxt_i[124:125, 1599:1600], dst[E - 1:E].rearrange("(a c) -> a c", a=1)).then_inc(s_dl, 16)
            e.dma_start(c[:, :], cst).then_inc(s_const, 16)
            for t, s in ((srcT, src), (dstT, dst), (ewT, ew)):
                e.dma_start(t[0:1562, :], s[0:1562 * 128].rearrange("(a b) -> a b", b=128)).then_inc(s_tab, 16)
                e.dma_start(t[1562:1563, 0:64], s[1562 * 128:E].rearrange("(a b) -> a b", a=1)).then_inc(s_tab, 16)
            e.wait_ge(s_pad, 3)
            for t, q in ((srcT, zer[:, 0:128].bitcast(i32)), (dstT, padi), (ewT, zer[:, 0:128])):
                e.dma_start(t[1562:1563, 64:128], q[0:1, 0:64]).then_inc(s_tab, 16)
                e.dma_start(t[1563:1664, :], q[0:101, :]).then_inc(s_tab, 16)
            for n, b in enumerate((b0.rearrange("(a o) h d -> a (o h d)", a=1), bm.rearrange("(a n) -> a n", a=1),
                                   bu.rearrange("(a n) -> a n", a=1))):
                e.dma_start(brow[0:3, n, :], b.to_broadcast([3, 256])).then_inc(s_w, 16)
            for k in range(2):
                for o in range(2):
                    e.dma_start(w0[:, k, o * 128:(o + 1) * 128].rearrange("p (h d) -> p h d", h=4),
                                W0[o, :, k * 128:(k + 1) * 128, :].rearrange("h p d -> p h d")).then_inc(s_w, 16)
            e.dma_start(wm[:, :, 0:256], Wm[0:256, :].rearrange("(k p) n -> p k n", p=128)).then_inc(s_w, 16)
            e.dma_start(wm[:, :, 256:512], Wm[256:512, :].rearrange("(k p) n -> p k n", p=128)).then_inc(s_w, 16)
            for o in range(2):
                e.dma_start(attb[:, o * 128:(o + 1) * 128].rearrange("p (h d) -> p h d", h=4),
                            att[0:1, :, o * 32:(o + 1) * 32].to_broadcast([128, 4, 32])).then_inc(s_w, 16)
            e.dma_start(scb[:, :], scale.rearrange("(a o) h d -> a (o h d)", a=1).to_broadcast([128, 256])).then_inc(s_w, 16)
            e.dma_start(ofb[:, :], offset.rearrange("(a o) h d -> a (o h d)", a=1).to_broadcast([128, 256])).then_inc(s_w, 16)

            def loadt(p, buf, j, g):
                waitn(e, p + "_mm", j - 3)
                if known(j, lambda j: j == NP - 1):
                    e.dma_start(buf[g % 4][:, :, 0:128 + LASTR],
                                xT.rearrange("(k p) n -> p k n", p=128)[:, :, j * 256:N]).then_inc(S(f"{p}_xt{g % 4}"), 16)
                else:
                    e.dma_start(buf[g % 4], xT.rearrange("(k p) n -> p k n", p=128)[:, :, bass.ds(j * 256, 256)])\
                     .then_inc(S(f"{p}_xt{g % 4}"), 16)
            loadt("a", XT0, 0, 0)
            loadt("a", XT0, 1, 1)

            e.wait_ge(s_A, A_TILE)
            e.dma_start(d_tile.rearrange("c p -> p c"), tI, allow_slow_non_contiguous=True).then_inc(s_tl, 16)
            e.wait_ge(s_tl, 16)
            e.dma_start(trow[:, :].rearrange("a (c p) -> a c p", c=NC), d_tile.rearrange("(a c) p -> a c p", a=1)).then_inc(s_tl, 16)

            def load(j, g, i):
                if not done(j + 2, NP):
                    loadt("a", XT0, j + 2, g + 2)
                for k in (2, 3):
                    e.dma_start(pair(acc[k], j), zer.unsqueeze(1).to_broadcast([128, 2, 256])).then_inc(S("zero2"), 16)
            drive(e, NP, 4, load, tail=5)
            e.wait_ge(S("a_mm"), NP)
            zeroed(e)

            loadt("d", XT0B, 0, 0)
            loadt("d", XT0B, 1, 1)

            def load2(j, g, i):
                if not done(j + 2, NP):
                    loadt("d", XT0B, j + 2, g + 2)
                if not done(j, NP):
                    waitn(e, f"d_st{g}", 16 * uses(i, g, 4, 4))
                    if known(j, lambda j: j == NP - 1):
                        e.dma_start(X0[g][:, 0, :], x[j * 256:j * 256 + 128, :]).then_inc(S(f"d_in{g}"), 16)
                        e.dma_start(X0[g][0:LASTR, 1, :], x[j * 256 + 128:N, :]).then_inc(S(f"d_in{g}"), 16)
                    else:
                        e.dma_start(X0[g], pair(x, j)).then_inc(S(f"d_in{g}"), 16)
                if not done(j, NP, 3):
                    waitn(e, "d_x", j - 2)
                    e.dma_start(pair(d_xp, j - 3), X0[(g - 3) % 4]).then_inc(S(f"d_st{(g - 3) % 4}"), 16)
            drive(e, NP + 3, 4, load2, tail=8)

            for g in range(4):
                e.wait_ge(S(f"d_st{g}"), 16 * (13 if g == 0 else 12))
            for k in range(4):
                e.wait_ge(S(f"e_sc{k}"), 16 * NG)

            def loada(j, g):
                waitn(e, "b_v", j - 3)
                for k in range(4):
                    e.dma_start(AC[g % 4][k], pair(acc[k], j)).then_inc(S(f"b_ac{g % 4}"), 16)
            e.wait_ge(S("e_dc"), 2 * NG)
            loada(0, 0)
            loada(1, 1)

            def loadb(j, g, i):
                h = g % 2
                if not done(j + 2, NP):
                    loada(j + 2, g + 2)
                if not done(j, NP):
                    waitn(e, "b_nm", 2 * (j - 3))
                    e.dma_start(X1[g], pair(d_xp, j)).then_inc(S(f"b_in{g}"), 16)
                if not done(j, NP, 4):
                    waitn(e, "b_nm", 2 * (j - 3))
                    e.dma_start(pair(d_x1, j - 4), XN[h]).then_inc(S(f"b_s1{h}"), 16)
                if not done(j, NP, 6):
                    waitn(e, "b_pq", 2 * (j - 5))
                    e.dma_start(pair(d_p, j - 6), PQ[h][:, :, 0:256]).then_inc(S(f"b_s3{h}"), 16)
                    e.dma_start(pair(d_q, j - 6), PQ[h][:, :, 256:512]).then_inc(S(f"b_s3{h}"), 16)
            drive(e, NP + 6, 4, loadb, head=2, tail=8)
            stored_b(e)

            e.dma_start(WU, Wu.rearrange("(k p) n -> p k n", p=128)).then_inc(s_w, 16)
            e.dma_start(GB, gam.rearrange("(a n) -> a n", a=1).to_broadcast([128, 256])).then_inc(s_w, 16)
            e.dma_start(BB, bet.rearrange("(a n) -> a n", a=1).to_broadcast([128, 256])).then_inc(s_w, 16)

            regs = [e.alloc_register(f"spt{k}") for k in range(4)]

            def loadq(j, g, i):
                e.load(regs, trow[0:1, bass.ds(j * 4, 4)])
                ts = [e.snap(r, min_val=0, max_val=NT - 1) for r in regs]
                waitn(e, "f_qe", j - 1)
                for k, t in enumerate(ts):
                    e.dma_start(Q1[g % 2][:, k, :], d_q[bass.ds(t * 128, 128), :]).then_inc(S(f"f_q{g}"), 16)
            drive(e, NG, 4, loadq)

            def loadx(j, g):
                waitn(e, "g_tr", j - 3)
                waitn(e, "g_xb", j - 3)
                e.dma_start(X2[g % 4], pair(d_x1, j)).then_inc(S(f"g_in{g % 4}"), 16)
            loadx(0, 0)
            loadx(1, 1)

            def loadg(j, g, i):
                h = g % 2
                if not done(j + 2, NP):
                    loadx(j + 2, g + 2)
                if not done(j, NP, 5):
                    waitn(e, "g_n2", 2 * (j - 4))
                    o = O2[1 - h]
                    if known(j, lambda j: j - 5 == NP - 1):
                        e.dma_start(out[(j - 5) * 256:(j - 5) * 256 + 128, :], o[:, 0, :]).then_inc(S(f"g_st{1 - h}"), 16)
                        e.dma_start(out[(j - 5) * 256 + 128:N, :], o[0:LASTR, 1, :]).then_inc(S(f"g_st{1 - h}"), 16)
                    else:
                        e.dma_start(pair(out, j - 5), o).then_inc(S(f"g_st{1 - h}"), 16)
            drive(e, NP + 5, 4, loadg, head=2, tail=8)
            e.wait_ge(S("g_st0"), 16 * 26)
            e.wait_ge(S("g_st1"), 16 * 24)

        @block.gpsimd
        def _(e):
            e.memset(zer, 0.0).then_inc(s_pad, 1)
            e.memset(padi, -1).then_inc(s_pad, 1)
            e.memset(ones[:, :], 1.0).then_inc(s_pad, 1)
            e.wait_ge(s_A, A_ROW)
            e.indirect_dma_start(out=row_i[0:NT + 1, :], out_offset=None, in_=dst.rearrange("(p c) -> p c", p=125),
                                 in_offset=bass.IndirectOffsetOnAxis(ap=ri[0:NT + 1, :], axis=0)).then_inc(S("Ar"), 16)
            e.wait_ge(s_tab, 16 * 12)
            e.wait_ge(s_A, A_FLAG)

            def place():
                e.dma_start(fsrc[0:125, :], src.rearrange("(p c) -> p c", p=125).bitcast(f32)).then_inc(S("u_l"), 16)
                e.dma_start(few[0:125, :], ew.rearrange("(p c) -> p c", p=125)).then_inc(S("u_l"), 16)

                def one(j, g, i):
                    waitn(e, "u_pi", j + 1)
                    waitn(e, "u_v", j + 1)
                    go(e)
                    for k, t in enumerate((dstT, srcT, ewT)):
                        v = fval[0:125, k:k + 1]
                        e.indirect_dma_start(out=t.rearrange("a (b o) -> (a b) o", o=1),
                                             out_offset=bass.IndirectOffsetOnAxis(ap=fpi[0:125, :], axis=0),
                                             in_=v if k == 2 else v.bitcast(i32), in_offset=None).then_inc(S(f"u_sc{k}"), 16)
                drive(e, 1600, 1, one)
                for k in range(3):
                    e.wait_ge(S(f"u_sc{k}"), 16 * 1600)
            unsorted(e, "pool_u", place)

            e.wait_ge(s_A, A_CHUNK)
            for k, (t, d) in enumerate(((dstT, gD.bitcast(i32)), (srcT, gS.bitcast(i32)), (ewT, gW))):
                for cc in range(NC):
                    e.indirect_dma_start(out=d[:, cc, :], out_offset=None, in_=t,
                                         in_offset=bass.IndirectOffsetOnAxis(ap=cI[:, cc:cc + 1], axis=0)).then_inc(S(f"Ag{k}"), 16)
            e.wait_ge(s_w, 16 * 13)

            def dense(j, g, i):
                h = g % 2
                waitn(e, "a_re", j + 1)
                waitn(e, "a_lk", j + 1)
                go(e)
                e.tensor_tensor(h4(big[:, bass.ds(2 * j, 2), 128:256]), h4(FN[h]),
                                bh(sm(g, 16, 8)).unsqueeze(3).to_broadcast(hb), ALU.mult).then_inc(S("a_gm"), 1)
            drive(e, NP, 4, dense, tail=1)

            zeroed(e)

            def scat(j, g, i):
                waitn(e, "e_dc", 2 * (j + 1))
                waitn(e, "e_ix", j + 1)
                for k in range(4):
                    waitn(e, f"e_sc{k}", j * 16)
                    go(e)
                    e.indirect_dma_start(out=acc[k], out_offset=bass.IndirectOffsetOnAxis(ap=idx[:, g, k:k + 1], axis=0),
                                         in_=DS[g % 2][:, k, :], in_offset=None, compute_op=ALU.add).then_inc(S(f"e_sc{k}"), 16)
            drive(e, NG, 4, scat)
            for k in range(4):
                e.wait_ge(S(f"e_sc{k}"), 16 * NG)

            e.wait_ge(S("e_dc"), 2 * NG)
            e.memset(ZB, 0.0).then_inc(S("b_zb"), 1)

            def dense1(j, g, i):
                if not done(j, NP):
                    waitn(e, f"b_ac{g}", 64 * uses(i, g, 0, 4))
                    e.tensor_tensor(AC[g][0], AC[g][0], AC[g][1], ALU.add).then_inc(S("b_a1"), 1)
                    e.tensor_tensor(AC[g][2], AC[g][2], AC[g][3], ALU.add).then_inc(S("b_a3"), 1)
                if not done(j, NP, 1):
                    q = (g - 1) % 4
                    waitn(e, f"b_in{q}", 16 * uses(i, g, 1, 4))
                    e.tensor_tensor(X1[q], X1[q], bc2(ofb[:, :]), ALU.add).then_inc(S("b_xo"), 1)
            drive(e, NP + 1, 4, dense1, tail=2)

            stored_b(e)

            def gath(j, g, i):
                waitn(e, "f_m", 2 * (j - 3))
                waitn(e, "f_ix", j + 1)
                go(e)
                for k in range(4):
                    e.indirect_dma_start(out=G1[g][:, k, :], out_offset=None, in_=d_p,
                                         in_offset=bass.IndirectOffsetOnAxis(ap=idx[:, g, k:k + 1], axis=0)).then_inc(S(f"f_g{g}"), 16)
            drive(e, NG, 4, gath)

            e.wait_ge(S("f_acc"), 4 * NG)
            e.wait_ge(s_w, 16 * 16)

            def sums(j, g, i):
                if not done(j, NP):
                    waitn(e, "g_tr", j - 1)
                    go(e)
                    e.tensor_copy(AG[g % 2], big[:, bass.ds(2 * j, 2), :]).then_inc(S("g_ag"), 1)
                if not done(j, NP, 1):
                    q = (g - 1) % 4
                    waitn(e, f"g_in{q}", 16 * uses(i, g, 1, 4))
                    waitn(e, "g_add", j - 4)
                    go(e)
                    e.tensor_tensor(XB[q], X2[q], bc2(BB), ALU.add).then_inc(S("g_xb"), 1)
            drive(e, NP + 1, 4, sums, head=2, tail=2)

        @block.scalar
        def _(e):
            e.wait_ge(s_pad, 3)
            e.wait_ge(s_dl, 64)
            e.wait_ge(s_tab, 16 * 12)
            e.wait_ge(s_w, 16 * 13)
            for n in range(14):
                k, a = n // 7, n % 7
                waitn(e, f"zero{n % 2}", 16 * (n // 2))
                e.dma_start(acc[k][a * 1792:(a + 1) * 1792, :].rearrange("(b p) c -> p b c", p=128),
                            zer.unsqueeze(1).to_broadcast([128, 14, 256])).then_inc(S(f"zero{n % 2}"), 16)

            for n, (kind, c0, c1) in enumerate(TABS):
                e.wait_ge(s_Ap, n + 3)
                e.activation(tab[:, c0 * 32:c1 * 32, kind, :],
                             PS[n % 2][:, 0:(c1 - c0) * 128].rearrange("p (a b) -> p a b", b=4), ACT.Copy).then_inc(s_At, 1)

            def dense(j, g, i):
                h = g % 2
                waitn(e, "a_fc", j)
                waitn(e, "a_gm", j - 1)
                waitn(e, "a_u", j - 1)
                waitn(e, "a_mm", j + 1)
                e.activation(FN[h], q2(PS[2 + h][:, 0:256]), ACT.Relu).then_inc(S("a_re"), 1)
                waitn(e, "a_re", j + 1)
                go(e)
                e.activation(big[:, bass.ds(2 * j, 2), 0:128], FN[h], ACT.Copy).then_inc(S("a_fc"), 1)
            drive(e, NP, 4, dense, tail=1)
            zeroed(e)

            def own(j, g, i):
                h = g % 2

                def square():
                    waitn(e, "d_rv", j - 2)
                    waitn(e, "d_xc", j)
                    e.activation(SQ0[1 - h], XC0[1 - h], ACT.Square).then_inc(S("d_s2"), 1)

                def relu():
                    waitn(e, "d_xc", j - 1)
                    waitn(e, "d_mm", j + 1)
                    e.activation(FS[h], q2(PS[3][:, 0:256]), ACT.Relu).then_inc(S("d_re"), 1)

                def root():
                    waitn(e, "d_var", j)
                    e.activation(sm(g - 1, 64, 8), sm(g - 1, 56, 8), ACT.Sqrt).then_inc(S("d_sq"), 1)
                p0, p1 = not done(j, NP), not done(j, NP, 1)
                return [[], [square] * p1, [relu] * p0, [], [], [], [], [root] * p1]

            def edge0(j, g, i):
                if not done(j, NG, 1):
                    waitn(e, "e_d", j - 2)
                    waitn(e, "e_c", j)
                    e.activation(CS[(g - 1) % 2], q4(PS[2][:, :]), ACT.Copy).then_inc(S("e_cc"), 1)
                if not done(j, NG, 2):
                    for k in range(4):
                        waitn(e, f"e_sc{k}", (j - 3) * 16)
                    waitn(e, "e_d", j - 1)
                    for h in range(2):
                        e.activation(DS[g % 2][:, 2 * h:2 * h + 2, :], q2(PS[4 + 2 * (g % 2) + h][:, :]), ACT.Copy)\
                         .then_inc(S("e_dc"), 1)
            drive(e, NG // 8, 4, merged(own, edge0), tail=4)
            for j in (NG, NG + 1):
                edge0(j, j % 4, None)

            flat = big[:, :, :].rearrange("p a b -> p (a b)")
            e.wait_ge(S("b_zb"), 1)

            def densb(j, g, i):
                h = g % 2
                if not done(j, NP, 2):
                    waitn(e, "b_var", j - 1)
                    e.activation(sm(g - 2, 64, 8), sm(g - 2, 56, 8), ACT.Sqrt).then_inc(S("b_sq"), 1)
                if not done(j, NP, 3):
                    waitn(e, "b_v2", j - 2)
                    e.activation(sm(g - 3, 100, 2), sm(g - 3, 98, 2), ACT.Sqrt).then_inc(S("b_sr"), 1)
                if not done(j, NP, 1):
                    waitn(e, "b_rv", j - 2)
                    waitn(e, "b_xc", j)
                    e.activation(SQ1[1 - h], XC1[1 - h], ACT.Square).then_inc(S("b_s2"), 1)
                if not done(j, NP, 4):
                    waitn(e, "b_tr", j - 3)
                    e.activation(XT1[h], q4(PS[h][:, :]), ACT.Copy).then_inc(S("b_xt"), 1)
                if not done(j, NP, 5):
                    waitn(e, f"b_s3{1 - h}", 32 * uses2(i, g, 7))
                    waitn(e, "b_mm", j - 4)
                    for b in range(2):
                        e.activation(PQ[1 - h][:, b, :], PS[2 + 2 * (1 - h) + b][:, :], ACT.Copy).then_inc(S("b_pq"), 1)
                if not done(j, NP, 3):
                    waitn(e, f"b_s1{1 - h}", 16 * uses2(i, g, 5))
                    waitn(e, "b_tr", j - 4)
                    waitn(e, "b_rn", j - 2)
                    for b in range(2):
                        e.activation(XN[1 - h][:, b, :], X1[(g - 3) % 4][:, b, :], ACT.Identity,
                                     bias=sm(g - 3, 104 + b, 1), scale=sm(g - 3, 102 + b, 1)).then_inc(S("b_nm"), 1)
                if not done(j, 48):
                    go(e)
                    e.activation(flat[:, bass.ds(j * ZN + NAC * 256, ZN)], ZB, ACT.Copy).then_inc(S("f_z"), 1)
            drive(e, NP + 5, 4, densb, head=2, tail=6)
            stored_b(e)

            def window1(j, g):
                e.activation(win[:, g % 4, :, :], tab[:, j, :, :], ACT.Copy).then_inc(S("f_win"), 1)
                e.activation(idx[:, g % 4, :], tab[:, j, 1, :], ACT.Copy).then_inc(S("f_ix"), 1)
            window1(0, 0)
            window1(1, 1)

            def edge1(j, g, i):
                if not done(j + 2, NG):
                    waitn(e, f"f_g{(g + 2) % 4}", 64 * uses(i, g, 2, 4))
                    waitn(e, "f_oh", j - 1)
                    go(e)
                    window1(j + 2, g + 2)
                if not done(j, NG):
                    waitn(e, "f_qe", j - 1)
                    waitn(e, "f_tr", j + 1)
                    e.activation(OT1[g % 2], q4(PS[g % 2][:, :]), ACT.Copy).then_inc(S("f_ot"), 1)
                if not done(j, NG, 1):
                    waitn(e, "f_m", 2 * j)
                    e.activation(M1[(g - 1) % 2], M1[(g - 1) % 2], ACT.Relu).then_inc(S("f_re"), 1)
            drive(e, NG + 1, 4, edge1, tail=5)

            e.wait_ge(S("f_acc"), 4 * NG)

            def densg(j, g, i):
                h = g % 2
                if not done(j, NP, 3):
                    waitn(e, "g_v1", j - 2)
                    e.activation(sm(g - 3, 100, 2), sm(g - 3, 98, 2), ACT.Sqrt).then_inc(S("g_sq"), 1)
                if not done(j, NP, 1):
                    waitn(e, "g_mm", j - 2)
                    waitn(e, "g_tr", j)
                    e.activation(XT2[1 - h], q4(PS[5 - h][:, :]), ACT.Copy)
                    e.activation(AT[1 - h], q4(PS[1 - h][:, :]), ACT.Copy).then_inc(S("g_at"), 1)
                if not done(j, NP, 4):
                    waitn(e, "g_v2", j - 3)
                    e.activation(sm(g - 4, 50, 2), sm(g - 4, 48, 2), ACT.Sqrt).then_inc(S("g_sr"), 1)
                if not done(j, NP, 2):
                    waitn(e, "g_n1", 2 * (j - 3))
                    waitn(e, "g_mm", j - 1)
                    e.activation(H2[h], q2(PS[2 + h][:, :]), ACT.Relu).then_inc(S("g_re"), 1)
                if not done(j, NP, 3):
                    waitn(e, "g_n2", 2 * (j - 4))
                    waitn(e, "g_rn", j - 2)
                    for b in range(2):
                        e.activation(N2[1 - h][:, b, :], H2[1 - h][:, b, :], ACT.Identity,
                                     bias=sm(g - 3, 104 + b, 1), scale=sm(g - 3, 102 + b, 1)).then_inc(S("g_n1"), 1)
                if not done(j, NP, 4):
                    waitn(e, f"g_st{h}", 16 * uses2(i, g, 6))
                    waitn(e, "g_rm", j - 3)
                    for b in range(2):
                        e.activation(O2[h][:, b, :], N2[h][:, b, :], ACT.Identity,
                                     bias=sm(g - 4, 54 + b, 1), scale=sm(g - 4, 52 + b, 1)).then_inc(S("g_n2"), 1)
            drive(e, NP + 4, 4, densg, head=2, tail=5)

        @block.tensor
        def _(e):
            e.wait_ge(s_pad, 3)
            e.wait_ge(s_A, A_M)
            e.matmul(PS[6][0:NT + 1, 0:1], before[0:125, 0:NT + 1], ones[0:125, 0:1], start=True, stop=True).then_inc(s_Ap, 1)
            e.wait_ge(s_const, 16)
            e.wait_ge(s_A, A_CNT)
            e.matmul(PS[7][:, 0:NT + 1], ones[0:NT + 1, :], diag[0:NT + 1, 0:NT + 1], start=True, stop=True)
            e.matmul(PS[7][:, NT + 1:NT + 2], ones[0:125, :], flag[0:125, :], start=True, stop=True).then_inc(s_Ap, 1)
            e.wait_ge(s_A, A_FLAG)

            def place():
                e.wait_ge(S("u_n"), U_CNT)
                e.matmul(PS[7][:, 0:NT + 1], ones[0:125, :], cnt[0:125, 0:NT + 1], start=True, stop=True).then_inc(S("u_m0"), 1)

                def one(j, g, i):
                    waitn(e, "u_b", j)
                    waitn(e, "u_o", j + 1)
                    e.matmul(PS[6][0:125, 0:NT], c[0:125, C_LT:C_LT + 125], fO[0:125, :], start=True, stop=True)
                    e.matmul(PS[6][:, 128:128 + NT], ones[0:125, :], fO[0:125, :], start=True, stop=True).then_inc(S("u_mm"), 1)
                drive(e, 1600, 1, one)
            unsorted(e, "pe_u", place)

            for n, (kind, c0, c1) in enumerate(TABS):
                if c0 == 0:
                    if kind < 2:
                        e.wait_ge(s_A, (A_LOC, A_LOC + 1)[kind])
                    else:
                        e.wait_ge(S("Ag2"), 16 * NC)
                wait(e, s_At, n - 1)
                for cc in range(c0, c1):
                    m = e.transpose(PS[n % 2][:, (cc - c0) * 128:(cc - c0 + 1) * 128], (gD, gS, gW)[kind][:, cc, :], ident)
                m.then_inc(s_Ap, 1)
            e.wait_ge(s_w, 16 * 13)
            e.wait_ge(s_A, A_BIAS)

            def bias(o, n):
                return e.matmul(o, onesb[0:3, :], b3[0:3, n, :], start=False, stop=True)

            def half(o, t, b, c0, n):
                for k in range(2):
                    e.matmul(o, t[:, k, b * 128:(b + 1) * 128], w0[:, k, c0:c0 + 128], start=(k == 0), stop=False)
                return e.matmul(o, onesb[0:3, :], b3[0:3, 0, c0:c0 + 128], start=False, stop=True)

            def dense(j, g, i):
                h = g % 2
                waitn(e, "a_re", j - 1)
                waitn(e, f"a_xt{g}", 16 * uses(i, g, 0, 4))
                for b in range(2):
                    m = half(PS[2 + h][:, b * 128:(b + 1) * 128], XT0[g], b, 128, 0)
                m.then_inc(S("a_mm"), 1)
            drive(e, NP, 4, dense, tail=1)

            e.wait_ge(s_tl, 32)
            e.wait_ge(S("a_fc"), NP)
            e.wait_ge(S("a_gm"), NP)

            def own(j, g, i):
                def product():
                    waitn(e, "d_re", j)
                    waitn(e, f"d_xt{g}", 16 * uses(i, g, 0, 4))
                    for b in range(2):
                        m = half(PS[3][:, b * 128:(b + 1) * 128], XT0B[g], b, 0, 0)
                    m.then_inc(S("d_mm"), 1)
                return [[product] * (not done(j, NP))] + [[]] * 7
            regs = [e.alloc_register(f"pet{k}") for k in range(4)]

            def edge0(j, g, i):
                if not done(j, NG):
                    waitn(e, "e_s", j - 1)
                    waitn(e, "e_win", j + 1)
                    for k in range(4):
                        m = e.transpose(PS[g % 2][:, k * 128:(k + 1) * 128],
                                        win[:, g % 2, 1, k:k + 1].to_broadcast([128, 128]), ident)
                    m.then_inc(S("e_r"), 1)
                if not done(j, NG, 1):
                    waitn(e, "e_cc", j - 1)
                    waitn(e, "e_oh", j)
                    waitn(e, "e_sw", j)
                    q = (g - 1) % 2
                    for k in range(4):
                        m = e.matmul(PS[2][:, k * 128:(k + 1) * 128], OH[q][:, k, :], SW[q][:, k, :], start=True, stop=True)
                    m.then_inc(S("e_c"), 1)
                if not done(j, NG, 2):
                    q = g % 2
                    e.load(regs, trow[0:1, bass.ds(j * 4 - 8, 4)])
                    ts = [e.snap(r, min_val=0, max_val=NT - 1) for r in regs]
                    waitn(e, "e_dc", 2 * (j - 3))
                    waitn(e, "e_cc", j - 1)
                    for k, t in enumerate(ts):
                        m = e.matmul(PS[4 + 2 * q + k // 2][:, (k % 2) * 256:(k % 2) * 256 + 256],
                                     CS[q][:, k, :], big[:, t, :], start=True, stop=True)
                    m.then_inc(S("e_d"), 1)
            drive(e, NG // 8, 4, merged(own, edge0), tail=4)
            for j in (NG, NG + 1):
                edge0(j, j % 4, None)

            def densb(j, g, i):
                h = g % 2
                if not done(j, NP, 4):
                    waitn(e, "b_pq", 2 * (j - 5))
                    waitn(e, "b_xt", j - 3)
                    for b in range(2):
                        o = PS[2 + 2 * h + b]
                        for k in range(2):
                            e.matmul(o[:, :], XT1[h][:, 2 * b + k, :], wm[:, k, :], start=(k == 0), stop=False)
                        m = bias(o[:, 0:256], 1)
                    m.then_inc(S("b_mm"), 1)
                if not done(j, NP, 3):
                    q = 1 - h
                    waitn(e, "b_xt", j - 4)
                    waitn(e, "b_nm", 2 * (j - 2))
                    for b in range(2):
                        for k in range(2):
                            m = e.transpose(PS[q][:, (2 * b + k) * 128:(2 * b + k + 1) * 128],
                                            XN[q][:, b, k * 128:(k + 1) * 128], ident)
                    m.then_inc(S("b_tr"), 1)
            drive(e, NP + 4, 4, densb, head=2, tail=5)
            e.wait_ge(S("b_pq"), 2 * NP)

            def edge1(j, g, i):
                if not done(j, NG):
                    waitn(e, "f_ot", j - 1)
                    waitn(e, "f_oh", j + 1)
                    for k in range(4):
                        m = e.transpose(PS[g % 2][:, k * 128:(k + 1) * 128], OH1[g][:, k, :], ident)
                    m.then_inc(S("f_tr"), 1)
                if not done(j, NG, 3):
                    q = (g - 3) % 2
                    waitn(e, "f_acc", 4 * (j - 4))
                    waitn(e, "f_re", j - 2)
                    for k in range(4):
                        m = e.matmul(PS[4 + 2 * q + k // 2][:, (k % 2) * 256:(k % 2) * 256 + 256],
                                     OH1[(g - 3) % 4][:, k, :], M1[q][:, k, :], start=True, stop=True)
                    m.then_inc(S("f_ag"), 1)
                if not done(j, NG, 1):
                    q = (g - 1) % 2
                    waitn(e, "f_m", 2 * (j - 1))
                    waitn(e, "f_ot", j)
                    waitn(e, f"f_q{(g - 1) % 4}", 64 * uses(i, g, 1, 4))
                    for k in range(4):
                        m = e.matmul(PS[2 + k // 2][:, (k % 2) * 256:(k % 2) * 256 + 256],
                                     OT1[q][:, k, :], Q1[q][:, k, :], start=True, stop=True)
                    m.then_inc(S("f_qe"), 1)
            drive(e, NG + 3, 4, edge1, head=2, tail=3)
            e.wait_ge(s_w, 16 * 16)

            def densg(j, g, i):
                h = g % 2
                if not done(j, NP):
                    waitn(e, "g_at", j - 1)
                    waitn(e, "g_ag", j + 1)
                    waitn(e, f"g_in{g}", 16 * uses(i, g, 0, 4))
                    for b in range(2):
                        for k in range(2):
                            e.transpose(PS[4 + h][:, (2 * b + k) * 128:(2 * b + k + 1) * 128],
                                        X2[g][:, b, k * 128:(k + 1) * 128], ident)
                    for b in range(2):
                        for k in range(2):
                            m = e.transpose(PS[h][:, (2 * b + k) * 128:(2 * b + k + 1) * 128],
                                            AG[h][:, b, k * 128:(k + 1) * 128], ident)
                    m.then_inc(S("g_tr"), 1)
                if not done(j, NP, 1):
                    q = 1 - h
                    waitn(e, "g_re", j - 2)
                    waitn(e, "g_at", j)
                    for b in range(2):
                        o = PS[2 + q][:, b * 256:(b + 1) * 256]
                        for k in range(2):
                            e.matmul(o, XT2[q][:, 2 * b + k, :], WU[:, k, :], start=(k == 0), stop=False)
                        for k in range(2):
                            e.matmul(o, AT[q][:, 2 * b + k, :], WU[:, 2 + k, :], start=False, stop=False)
                        m = bias(o, 2)
                    m.then_inc(S("g_mm"), 1)
            drive(e, NP + 1, 4, densg, tail=2)

        @block.vector
        def _(e):
            n = [0]

            def A1(ins):
                n[0] += 1
                ins.then_inc(s_A, 1)
                e.wait_ge(s_A, n[0])

            e.wait_ge(s_const, 16)
            A1(e.tensor_scalar(thr, c[:, C_PID:C_PID + 1], 128.0, None, ALU.mult))
            e.wait_ge(s_dl, 64)
            A1(e.tensor_copy(first[0:125, :], dst_i[0:125, 0:1]))
            A1(e.tensor_scalar(before[0:125, :], c[0:125, C_IO:C_IO + 100], 128.0, first[0:125, :], ALU.mult, ALU.is_gt))
            assert n[0] == A_M
            e.wait_ge(s_Ap, 1)
            A1(e.tensor_scalar(rows[0:NT + 1, :], PS[6][0:NT + 1, 0:1], -1.0, 0.0, ALU.add, ALU.max))
            A1(e.tensor_copy(ri[0:NT + 1, :], rows[0:NT + 1, :]))
            assert n[0] == A_ROW
            A1(e.tensor_tensor(junk[0:125, :], dst_i[0:125, :], nxt_i[0:125, :], ALU.is_gt))
            A1(e.tensor_reduce(flag[0:125, :], junk[0:125, :], AX.X, ALU.add))
            e.wait_ge(s_w, 16 * 13)
            A1(e.memset(onesb[:, :], 1.0))
            A1(e.memset(bsum[0:3], 0.0))
            for k in range(3):
                A1(e.tensor_copy(bbf[0:3], brow[0:3]))
                A1(e.tensor_copy(bpart[0:3], bbf[0:3]))
                A1(e.tensor_tensor(brow[0:3], brow[0:3], bpart[0:3], ALU.subtract))
                A1(e.tensor_scalar(brem[0:3], bpart[0:3], c[0:3, C_ID + k:C_ID + k + 1], None, ALU.mult))
                A1(e.tensor_tensor(bsum[0:3], bsum[0:3], brem[0:3], ALU.add))
            A1(e.tensor_copy(b3[:, :, :], bsum[0:3]))
            assert n[0] == A_BIAS
            e.wait_ge(S("Ar"), 16)
            A1(e.tensor_copy(junk2[0:NT + 1, :], row_i[0:NT + 1, :]))
            A1(e.tensor_scalar(junk[0:NT + 1, :], junk2[0:NT + 1, :], thr[0:NT + 1, :], 0.0, ALU.is_lt, ALU.add,
                               accum_out=part[0:NT + 1, :]))
            A1(e.scalar_tensor_tensor(lower[0:NT + 1, :], rows[0:NT + 1, :], 1600.0, part[0:NT + 1, :], ALU.mult, ALU.add))
            A1(e.tensor_scalar(diag[0:NT + 1, :], c[0:NT + 1, C_ID:C_ID + 100], lower[0:NT + 1, :], None, ALU.mult))
            assert n[0] == A_CNT
            e.wait_ge(s_Ap, 2)
            A1(e.tensor_copy(st, PS[7][:, 0:100]))
            A1(e.tensor_copy(st_i, st))
            assert n[0] == A_FLAG

            def place():
                m = [0]

                def U1(ins):
                    m[0] += 1
                    ins.then_inc(S("u_n"), 1)
                    e.wait_ge(S("u_n"), m[0])

                U1(e.tensor_scalar(sid_i[0:125, :], dst_i[0:125, :], 7, None, ALU.arith_shift_right))
                U1(e.tensor_copy(tid_f[0:125, :], sid_i[0:125, :]))
                U1(e.memset(cnt[:, :], 0.0))
                for t in range(1, NT):
                    U1(e.tensor_scalar(junk[0:125, :], tid_f[0:125, :], float(t), 0.0, ALU.is_lt, ALU.add,
                                       accum_out=cnt[0:125, t:t + 1]))
                U1(e.memset(cnt[0:125, NT:NT + 1], float(E // 125)))
                assert m[0] == U_CNT
                e.wait_ge(S("u_m0"), 1)
                U1(e.tensor_copy(st[:, 0:NT + 1], PS[7][:, 0:NT + 1]))
                U1(e.tensor_copy(st_i[:, 0:NT + 1], st[:, 0:NT + 1]))
                U1(e.tensor_copy(fB, st[:, 0:NT]))
                e.wait_ge(S("u_l"), 32)

                def one(j, g, i):
                    e.tensor_copy(fcol[0:125, :], tid_f[0:125, bass.ds(j, 1)]).then_inc(S("u_c"), 1)
                    waitn(e, "u_c", j + 1)
                    e.tensor_scalar(fO[0:125, :], c[0:125, C_IO:C_IO + NT], fcol[0:125, :], None, ALU.is_equal).then_inc(S("u_o"), 1)
                    for k in range(3):
                        waitn(e, f"u_sc{k}", j * 16)
                    go(e)
                    e.tensor_copy(fval[0:125, 0:1].bitcast(i32), dst_i[0:125, bass.ds(j, 1)])
                    e.tensor_copy(fval[0:125, 1:2], fsrc[0:125, bass.ds(j, 1)])
                    e.tensor_copy(fval[0:125, 2:3], few[0:125, bass.ds(j, 1)]).then_inc(S("u_v"), 1)
                    waitn(e, "u_mm", j + 1)
                    e.tensor_tensor(fR[0:125, :], PS[6][0:125, 0:NT], fB[0:125, :], ALU.add).then_inc(S("u_r"), 1)
                    waitn(e, "u_r", j + 1)
                    e.tensor_tensor(fM[0:125, :], fR[0:125, :], fO[0:125, :], ALU.mult).then_inc(S("u_p"), 1)
                    e.tensor_tensor(fB, fB, PS[6][:, 128:128 + NT], ALU.add).then_inc(S("u_b"), 1)
                    waitn(e, "u_p", j + 1)
                    e.tensor_reduce(fpos[0:125, :], fM[0:125, :], AX.X, ALU.add).then_inc(S("u_q"), 1)
                    waitn(e, "u_q", j + 1)
                    e.tensor_copy(fpi[0:125, :], fpos[0:125, :]).then_inc(S("u_pi"), 1)
                    waitn(e, "u_pi", j + 1)
                    waitn(e, "u_b", j + 1)
                    go(e)
                drive(e, 1600, 1, one)
            unsorted(e, "dve_u", place)

            A1(e.tensor_scalar(fi_i, st_i, 7, None, ALU.arith_shift_right))
            A1(e.tensor_scalar(bA, st, 127.0, None, ALU.add))
            A1(e.tensor_copy(la_i, bA))
            A1(e.tensor_scalar(le_i, la_i, 7, None, ALU.arith_shift_right))
            A1(e.tensor_copy(fi, fi_i))
            A1(e.tensor_copy(la, le_i))
            A1(e.tensor_tensor(ne[:, 0:NT], st[:, 1:NT + 1], st[:, 0:NT], ALU.is_gt))
            A1(e.tensor_tensor(dC[:, 0:NT], la[:, 1:NT + 1], fi[:, 0:NT], ALU.subtract))
            A1(e.memset(bA, 0.0))
            A1(e.tensor_tensor(bA[:, 1:NT], dC[:, 0:NT - 1], ne[:, 0:NT - 1], ALU.mult))
            a, b = bA, bB
            for k in range(7):
                d = 1 << k
                A1(e.tensor_copy(b[:, 0:d], a[:, 0:d]))
                A1(e.tensor_tensor(b[:, d:NT], a[:, d:NT], a[:, 0:NT - d], ALU.add))
                a, b = b, a
            A1(e.tensor_tensor(la[:, 0:NT], fi[:, 0:NT], a[:, 0:NT], ALU.subtract))
            A1(e.tensor_tensor(dC[:, 1:NT], la[:, 1:NT], la[:, 0:NT - 1], ALU.subtract))
            b13 = [128, NC, NT - 1]
            A1(e.tensor_tensor(g13[:, :, 0:NT - 1], a[:, 1:NT].unsqueeze(1).to_broadcast(b13),
                               c[:, C_STEP:C_STEP + NC].unsqueeze(2).to_broadcast(b13), ALU.is_le))
            A1(e.tensor_tensor(h13[:, :, 0:NT - 1], g13[:, :, 0:NT - 1], dC[:, 1:NT].unsqueeze(1).to_broadcast(b13), ALU.mult))
            A1(e.tensor_reduce(tS, g13[:, :, 0:NT - 1], AX.X, ALU.add))
            A1(e.tensor_reduce(cS, h13[:, :, 0:NT - 1], AX.X, ALU.add))
            A1(e.tensor_copy(tI, tS))
            A1(e.tensor_tensor(tfl, cS, c[:, C_STEP:C_STEP + NC], ALU.add))
            A1(e.tensor_scalar(cS, tfl, float(CH), None, ALU.min))
            A1(e.tensor_copy(cI, cS))
            assert n[0] == A_CHUNK
            A1(e.tensor_scalar(tfl, tS, 128.0, None, ALU.mult))
            e.wait_ge(S("Ag0"), 16 * NC)
            A1(e.tensor_tensor(gD, gD.bitcast(i32), tfl.unsqueeze(2).to_broadcast([128, NC, 128]), ALU.subtract))
            assert n[0] == A_LOC
            e.wait_ge(S("Ag1"), 16 * NC)
            A1(e.tensor_copy(gS, gS.bitcast(i32)))

            e.wait_ge(s_At, len(TABS))
            e.tensor_scalar(tab[:, :, 3, :], tab[:, :, 1, :], c[:, C_DUMP:C_DUMP + 1], -1.0, ALU.subtract, ALU.mult).then_inc(s_At, 1)
            e.wait_ge(s_At, len(TABS) + 1)
            def dense(j, g, i):
                h = g % 2
                waitn(e, "a_ar", j)
                waitn(e, "a_re", j + 1)
                e.tensor_tensor(UN, FN[h], bc2(attb[:, 128:256]), ALU.mult).then_inc(S("a_u"), 1)
                waitn(e, "a_u", j + 1)
                e.tensor_reduce(bh(sm(g, 0, 8)), h4(UN), AX.X, ALU.add).then_inc(S("a_ar"), 1)
                waitn(e, "a_gm", j - 3)
                waitn(e, "a_ar", j + 1)
                e.scalar_tensor_tensor(sm(g, 16, 8), sm(g, 0, 8), 0.2, sm(g, 0, 8), ALU.mult, ALU.max).then_inc(S("a_lk"), 1)
            drive(e, NP, 4, dense, tail=1)

            def own(j, g, i):
                h = g % 2

                def deviation():
                    waitn(e, "d_sq", j - 1)
                    e.reciprocal(sm(g - 2, 72, 8), sm(g - 2, 64, 8)).then_inc(S("d_rc"), 1)
                    waitn(e, "d_sc", j - 2)
                    waitn(e, "d_rc", j - 1)
                    e.tensor_tensor(h4(Z0), h4(XC0[h]), bh(sm(g - 2, 72, 8)).unsqueeze(3).to_broadcast(hb), ALU.mult)\
                     .then_inc(S("d_z"), 1)

                def scaled():
                    waitn(e, "d_x", j - 2)
                    waitn(e, "d_z", j - 1)
                    e.tensor_tensor(Y0, Z0, bc2(scb[:, 0:128]), ALU.mult).then_inc(S("d_sc"), 1)

                def added():
                    q = (g - 2) % 4
                    waitn(e, f"d_in{q}", 16 * uses(i, g, 2, 4) + (16 if known(j, lambda j: j - 2 == NP - 1) else 0))
                    waitn(e, "d_sc", j - 1)
                    x0 = X0[q][:, :, 0:128]
                    e.tensor_tensor(x0, x0, Y0, ALU.add).then_inc(S("d_x"), 1)

                def attention():
                    waitn(e, "d_ar", j)
                    waitn(e, "d_re", j + 1)
                    e.tensor_tensor(US, FS[h], bc2(attb[:, 0:128]), ALU.mult).then_inc(S("d_u"), 1)

                def attention_sum():
                    waitn(e, "d_u", j + 1)
                    e.tensor_reduce(bh(sm(g, 0, 8)), h4(US), AX.X, ALU.add).then_inc(S("d_ar"), 1)

                def squares():
                    waitn(e, "d_s2", j)
                    e.tensor_reduce(bh(sm(g - 1, 48, 8)), h4(SQ0[1 - h]), AX.X, ALU.add).then_inc(S("d_rv"), 1)

                def head_sums():
                    e.tensor_reduce(bh(sm(g, 32, 8)), h4(FS[h]), AX.X, ALU.add).then_inc(S("d_hs"), 1)
                    waitn(e, "d_ar", j + 1)
                    e.scalar_tensor_tensor(sm(g, 16, 8), sm(g, 0, 8), 0.2, sm(g, 0, 8), ALU.mult, ALU.max).then_inc(S("d_lk"), 1)

                def variance():
                    waitn(e, "d_rv", j)
                    e.tensor_scalar(sm(g - 1, 56, 8), sm(g - 1, 48, 8), 1.0 / 32, 1e-9, ALU.mult, ALU.add).then_inc(S("d_var"), 1)

                def means():
                    waitn(e, "d_hs", j + 1)
                    e.tensor_scalar(sm(g, 40, 8), sm(g, 32, 8), 1.0 / 32, None, ALU.mult).then_inc(S("d_me"), 1)
                    waitn(e, "d_lk", j + 1)
                    go(e)
                    e.tensor_copy(ats[:, bass.ds(2 * j, 2), :], bh(sm(g, 16, 8))).then_inc(S("d_as"), 1)

                def centred():
                    waitn(e, "d_z", j - 1)
                    waitn(e, "d_me", j + 1)
                    e.tensor_tensor(h4(XC0[h]), h4(FS[h]), bh(sm(g, 40, 8)).unsqueeze(3).to_broadcast(hb), ALU.subtract)\
                     .then_inc(S("d_xc"), 1)
                p0, p1, p2 = (not done(j, NP, k) for k in range(3))
                return [[deviation] * p2, [scaled] * p2, [added] * p2, [attention] * p0, [attention_sum] * p0 + [squares] * p1,
                        [head_sums] * p0 + [variance] * p1, [means] * p0, [centred] * p0]

            e.wait_ge(S("a_gm"), NP)
            e.wait_ge(S("a_fc"), NP)
            zeroed(e)

            def window(j, g):
                e.tensor_copy(win[:, g % 2, :, :], tab[:, j, :, :]).then_inc(S("e_win"), 1)

            window(0, 0)

            def edge0(j, g, i):
                q = g % 2
                waitn(e, "e_c", j - 1)
                waitn(e, "e_win", j + 1)
                e.tensor_tensor(OH[q], iota.unsqueeze(1).to_broadcast(b4),
                                win[:, q, 0, :].unsqueeze(2).to_broadcast(b4), ALU.is_equal).then_inc(S("e_oh"), 1)
                waitn(e, "e_r", j + 1)
                e.tensor_tensor(SS, q4(PS[q][:, :]), win[:, q, 1, :].unsqueeze(2).to_broadcast(b4), ALU.is_equal).then_inc(S("e_s"), 1)
                if not done(j + 1, NG):
                    waitn(e, "e_ix", j)
                    go(e)
                    window(j + 1, g + 1)
                waitn(e, "e_s", j + 1)
                e.tensor_tensor(TT, SS, ltri.unsqueeze(1).to_broadcast(b4), ALU.mult).then_inc(S("e_tt"), 1)
                e.tensor_tensor(SW[q], SS, win[:, q, 2, :].unsqueeze(2).to_broadcast(b4), ALU.mult).then_inc(S("e_sw"), 1)
                waitn(e, "e_tt", j + 1)
                ct = sm(0, 96, 4)
                e.tensor_reduce(ct, TT, AX.X, ALU.add).then_inc(S("e_ct"), 1)
                waitn(e, "e_ct", j + 1)
                e.scalar_tensor_tensor(sm(0, 100, 4), ct, 0.5, win[:, q, 3, :], ALU.is_gt, ALU.mult).then_inc(S("e_fl"), 1)
                waitn(e, "e_fl", j + 1)
                for k in range(4):
                    waitn(e, f"e_sc{k}", (j - 3) * 16)
                e.tensor_tensor(idx[:, g, :], sm(0, 100, 4), win[:, q, 1, :], ALU.add).then_inc(S("e_ix"), 1)
            drive(e, NG // 8, 4, merged(own, edge0), tail=4)
            for k in range(4):
                e.wait_ge(S(f"e_sc{k}"), 16 * NG)

            def densb(j, g, i):
                h = g % 2
                p0, p1, p2, p3 = (not done(j, NP, k) for k in (0, 1, 2, 3))
                if p0:
                    waitn(e, "b_y", j)
                    waitn(e, "b_v", j)
                    waitn(e, "b_a1", j + 1)
                    waitn(e, "b_a3", j + 1)
                    e.tensor_tensor(SA, AC[g][0], AC[g][2], ALU.add).then_inc(S("b_a"), 1)
                if p3:
                    waitn(e, "b_sr", j - 2)
                    e.reciprocal(sm(g - 3, 102, 2), sm(g - 3, 100, 2)).then_inc(S("b_r2"), 1)
                if p0:
                    waitn(e, "b_a", j + 1)
                    go(e)
                    e.tensor_tensor(h4(YB), h4(SA[:, :, 0:128]), ats[:, bass.ds(2 * j, 2), :].unsqueeze(3).to_broadcast(hb), ALU.mult)\
                     .then_inc(S("b_y"), 1)
                if p3:
                    waitn(e, "b_r2", j - 2)
                    e.scalar_tensor_tensor(sm(g - 3, 104, 2), sm(g - 3, 92, 4).rearrange("p (b t) -> p b t", t=2)[:, :, 0], -1.0,
                                           sm(g - 3, 102, 2), ALU.mult, ALU.mult).then_inc(S("b_rn"), 1)
                if p1:
                    waitn(e, "b_s2", j)
                    e.tensor_reduce(bh(sm(g - 1, 48, 8)), h4(SQ1[1 - h]), AX.X, ALU.add).then_inc(S("b_rv"), 1)
                if p1:
                    waitn(e, "b_rv", j)
                    e.tensor_scalar(sm(g - 1, 56, 8), sm(g - 1, 48, 8), 1.0 / 32, 1e-9, ALU.mult, ALU.add).then_inc(S("b_var"), 1)
                if p2:
                    waitn(e, "b_sq", j - 1)
                    e.reciprocal(sm(g - 2, 72, 8), sm(g - 2, 64, 8)).then_inc(S("b_rc"), 1)
                if p0:
                    waitn(e, "b_xc", j)
                    waitn(e, "b_y", j + 1)
                    e.tensor_tensor(VV, YB, SA[:, :, 128:256], ALU.add).then_inc(S("b_v"), 1)
                if p2:
                    waitn(e, "b_rc", j - 1)
                    e.tensor_tensor(h4(Z1), h4(XC1[h]), bh(sm(g - 2, 72, 8)).unsqueeze(3).to_broadcast(hb), ALU.mult)\
                     .then_inc(S("b_z"), 1)
                if p0:
                    waitn(e, "b_v", j + 1)
                    e.tensor_reduce(bh(sm(g, 32, 8)), h4(VV), AX.X, ALU.add).then_inc(S("b_hs"), 1)
                if p2:
                    waitn(e, "b_z", j - 1)
                    e.tensor_tensor(Z2, Z1, bc2(scb[:, 128:256]), ALU.mult).then_inc(S("b_sc"), 1)
                if p0:
                    waitn(e, "b_hs", j + 1)
                    e.tensor_scalar(sm(g, 40, 8), sm(g, 32, 8), 1.0 / 32, None, ALU.mult).then_inc(S("b_me"), 1)
                if p2:
                    waitn(e, "b_xo", j - 1)
                    waitn(e, "b_sc", j - 1)
                    x1 = X1[(g - 2) % 4]
                    e.tensor_tensor(x1[:, :, 128:256], x1[:, :, 128:256], Z2, ALU.add).then_inc(S("b_x"), 1)
                if p0:
                    waitn(e, "b_me", j + 1)
                    e.tensor_tensor(h4(XC1[h]), h4(VV), bh(sm(g, 40, 8)).unsqueeze(3).to_broadcast(hb), ALU.subtract)\
                     .then_inc(S("b_xc"), 1)
                if p2:
                    waitn(e, "b_x", j - 1)
                    for b in range(2):
                        e.bn_stats(sm(g - 2, 80 + 6 * b, 6), x1[:, b, :]).then_inc(S("b_bn"), 1)
                if p2:
                    waitn(e, "b_bn", 2 * (j - 1))
                    go(e)
                    for b in range(2):
                        e.bn_aggr(sm(g - 2, 92 + 2 * b, 2), sm(g - 2, 80 + 6 * b, 6)).then_inc(S("b_ag"), 1)
                    waitn(e, "b_ag", 2 * (j - 1))
                    e.tensor_scalar(sm(g - 2, 98, 2), sm(g - 2, 92, 4).rearrange("p (b t) -> p b t", t=2)[:, :, 1], 1e-5, None, ALU.add)\
                     .then_inc(S("b_v2"), 1)
            drive(e, NP + 3, 4, densb, tail=4)

            e.wait_ge(S("b_v"), NP)
            e.memset(big[:, 0:NAC, :], 0.0).then_inc(S("f_z"), 1)
            e.wait_ge(S("f_z"), 1 + 48)
            stored_b(e)
            regs = [e.alloc_register(f"dvt{k}") for k in range(4)]

            def onehot(j, g):
                waitn(e, "f_ag", j - 3)
                waitn(e, "f_win", j + 1)
                e.tensor_tensor(OH1[g % 4], iota.unsqueeze(1).to_broadcast(b4),
                                win[:, g % 4, 0, :].unsqueeze(2).to_broadcast(b4), ALU.is_equal).then_inc(S("f_oh"), 1)
            onehot(0, 0)

            def edge1(j, g, i):
                p1, p4 = not done(j, NG, 1), not done(j, NG, 4)
                if p4:
                    e.load(regs, trow[0:1, bass.ds(j * 4 - 16, 4)])
                    ts = [e.snap(r, min_val=0, max_val=NT - 1) for r in regs]
                    waitn(e, "f_ag", j - 3)
                q = (g - 4) % 2

                def add(k):
                    if p4:
                        waitn(e, "f_acc", (j - 4) * 4 + k)
                        e.tensor_tensor(big[:, ts[k], :], big[:, ts[k], :],
                                        PS[4 + 2 * q + k // 2][:, (k % 2) * 256:(k % 2) * 256 + 256], ALU.add).then_inc(S("f_acc"), 1)

                def message(h):
                    if p1:
                        p = (g - 1) % 2
                        if h == 0:
                            waitn(e, "f_ag", j - 2)
                            waitn(e, "f_qe", j)
                            waitn(e, f"f_g{(g - 1) % 4}", 64 * uses(i, g, 1, 4))
                        e.tensor_tensor(M1[p][:, 2 * h:2 * h + 2, :], G1[(g - 1) % 4][:, 2 * h:2 * h + 2, :],
                                        q2(PS[2 + h][:, :]), ALU.add).then_inc(S("f_m"), 1)
                for k in range(4):
                    add(k)
                if not done(j + 1, NG):
                    onehot(j + 1, g + 1)
                message(0)
                message(1)
            drive(e, NG + 4, 4, edge1, head=2, tail=8)

            e.wait_ge(S("f_acc"), 4 * NG)
            e.wait_ge(s_w, 16 * 16)

            def densg(j, g, i):
                h = g % 2
                p2, p3 = not done(j, NP, 2), not done(j, NP, 3)

                def stats(p, lag, buf, base, name):
                    if p:
                        for b in range(2):
                            e.bn_stats(sm(g - lag, base + 6 * b, 6), buf[:, b, :]).then_inc(S(name), 1)

                def aggr(p, lag, base, to, name, src_name):
                    if p:
                        waitn(e, src_name, 2 * (j - lag + 1))
                        go(e)
                        for b in range(2):
                            e.bn_aggr(sm(g - lag, to + 2 * b, 2), sm(g - lag, base + 6 * b, 6)).then_inc(S(name), 1)

                def var(p, lag, mv, to, name, src_name):
                    if p:
                        waitn(e, src_name, 2 * (j - lag + 1))
                        e.tensor_scalar(sm(g - lag, to, 2), sm(g - lag, mv, 4).rearrange("p (b t) -> p b t", t=2)[:, :, 1], 1e-5, None,
                                        ALU.add).then_inc(S(name), 1)

                def factors(p, lag, mv, sq, rc, rn, names):
                    if p:
                        waitn(e, names[0], j - lag + 1)
                        e.reciprocal(sm(g - lag, rc, 2), sm(g - lag, sq, 2)).then_inc(S(names[1]), 1)
                        waitn(e, names[1], j - lag + 1)
                        e.scalar_tensor_tensor(sm(g - lag, rn, 2), sm(g - lag, mv, 4).rearrange("p (b t) -> p b t", t=2)[:, :, 0], -1.0,
                                               sm(g - lag, rc, 2), ALU.mult, ALU.mult).then_inc(S(names[2]), 1)
                factors(p3, 3, 92, 100, 102, 104, ("g_sq", "g_r1", "g_rn"))
                factors(not done(j, NP, 4), 4, 12, 50, 52, 54, ("g_sr", "g_r2", "g_rm"))
                if p2:
                    waitn(e, "g_re", j - 1)
                stats(p2, 2, H2[h], 80, "g_b1")
                if p3:
                    waitn(e, "g_n1", 2 * (j - 2))
                    n2 = N2[1 - h]
                    e.tensor_tensor(n2, n2, bc2(GB), ALU.mult).then_inc(S("g_gm"), 1)
                aggr(p2, 2, 80, 92, "g_a1", "g_b1")
                if p3:
                    waitn(e, "g_xb", j - 2)
                    waitn(e, "g_gm", j - 2)
                    e.tensor_tensor(n2, n2, XB[(g - 3) % 4], ALU.add).then_inc(S("g_add"), 1)
                var(p2, 2, 92, 98, "g_v1", "g_a1")
                if p3:
                    waitn(e, "g_add", j - 2)
                stats(p3, 3, N2[1 - h], 0, "g_b2")
                aggr(p3, 3, 0, 12, "g_a2", "g_b2")
                var(p3, 3, 12, 48, "g_v2", "g_a2")
            drive(e, NP + 4, 4, densg, tail=5)


AW = 13600
A_M = 3
A_ROW = A_M + 2
A_BIAS = A_ROW + 2 + 2 + 15 + 1
A_CNT = A_BIAS + 4
A_FLAG = A_CNT + 2
A_TILE = A_FLAG + 10 + 14 + 2 + 4 + 1
A_CHUNK = A_TILE + 3
A_LOC = A_CHUNK + 2
U_CNT = 3 + (NT - 1) + 1

_INS = ['x', 'xT', 'src', 'dst', 'edge_weight', 'L0_gnn_W', 'L0_gnn_b', 'L0_gnn_att', 'L0_gnn_scale', 'L0_gnn_offset',
        'L1_gnn_W_msg', 'L1_gnn_b_msg', 'L1_gnn_W_upd', 'L1_gnn_b_upd', 'L1_gnn_gamma', 'L1_gnn_beta']


def constants():
    import numpy as np
    c = np.zeros((128, CW), np.float32)
    p = np.arange(128, dtype=np.float32)
    c[:, C_ID:C_ID + 128] = np.eye(128)
    c[:, C_IO:C_IO + 128] = p[None, :]
    c[:, C_LT:C_LT + 128] = p[None, :] < p[:, None]
    c[:, C_PID] = p
    c[:, C_STEP:C_STEP + NC] = p[:, None] + 128 * np.arange(NC, dtype=np.float32)[None, :]
    c[:, C_DUMP] = NROW + p
    return c


def kernel(**inputs):
    import numpy as _np
    import concourse.bacc as _bacc
    from concourse import mybir as _mybir
    from concourse.bass_utils import run_bass_kernel_spmd as _run

    nc = _bacc.Bacc("TRN2", target_bir_lowering=False, num_devices=1)
    arrays, args = {}, []
    for name in _INS:
        a = _np.ascontiguousarray(inputs["x"].T if name == "xT" else inputs[name])
        arrays[f"in_{name}_dram"] = a
        args.append(nc.dram_tensor(f"in_{name}_dram", a.shape, _mybir.dt.from_np(a.dtype), kind="ExternalInput").ap())
    a = constants()
    arrays["in_cst_dram"] = a
    args.append(nc.dram_tensor("in_cst_dram", a.shape, _mybir.dt.from_np(a.dtype), kind="ExternalInput").ap())
    args.append(nc.dram_tensor("out_0_dram", (N, 256), f32, kind="ExternalOutput").ap())
    gnn(nc, *args)
    r = _run(nc, [arrays], core_ids=[0])
    return r.results[0]["out_0_dram"]
```
